# Optimizing a Trainium2 kernel written in Bass

```python
import numpy as np
import jax
import jax.numpy as jnp

def _softmax(x, axis=-1):
    return jax.nn.softmax(x, axis=axis)

def _gelu(x):
    return jax.nn.gelu(x, approximate=True)

def _silu(x):
    return jax.nn.silu(x)

def _sigmoid(x):
    return jax.nn.sigmoid(x)

def _layernorm(x, axis=-1, eps=1e-05):
    m = jnp.mean(x, axis=axis, keepdims=True)
    v = jnp.var(x, axis=axis, keepdims=True)
    return (x - m) / jnp.sqrt(v + eps)

def _scatter_add(tgt, idx, src, axis=0):
    return tgt.at[idx].add(src)

def _segment_sum(src, seg, n):
    return jax.ops.segment_sum(src, seg, n)
kernel_name = 'mk_adj_preln_d4_adj_r2_6afa8f'

def setup_inputs(seed: int=0):
    np.random.seed(seed)
    _w = jnp.asarray

    def _rec_inputs():
        import jax
        import jax.numpy as jnp
        _gk = jax.random.key(seed)
        x = -0.0002928 + 1 * jax.random.normal(jax.random.fold_in(_gk, 1), (128, 128, 256), jnp.float32)
        _w = (1.0 + jnp.arange(128, dtype=jnp.float32)) ** (-0.5)
        _w = _w / _w.mean()
        _pij = jnp.clip(0.125 * _w[:, None] * _w[None, :], 0.0, 1.0)
        _a = jax.random.uniform(jax.random.fold_in(_gk, 2), (128, 128, 128)) < _pij
        _a = jnp.logical_or(_a, jnp.swapaxes(_a, -1, -2))
        _a = jnp.logical_or(_a, jnp.eye(128, dtype=bool))
        _af = _a.astype(jnp.float32)
        _af = _af * jax.random.uniform(jax.random.fold_in(_gk, 3), (128, 128, 128), jnp.float32, 0.05, 1)
        adj = _af
        return (x, adj)
    x, adj = _rec_inputs()

    def _L0_gnn_setup():
        import jax, jax.numpy as jnp
        import numpy as np
        B, N, DIN, DOUT, K = (4, 1024, 256, 256, 3)
        key = jax.random.key(seed)
        ks = jax.random.split(key, 8)
        X = jax.random.normal(ks[0], (B, N, DIN), dtype=jnp.float32)
        A = jax.random.uniform(ks[1], (B, N, N), dtype=jnp.float32)
        Wv = jax.random.normal(ks[2], (DIN, DOUT), dtype=jnp.float32) * 0.02
        bv = jax.random.normal(ks[3], (DOUT,), dtype=jnp.float32) * 0.02
        aw = jax.random.normal(ks[4], (2 * DOUT, 1), dtype=jnp.float32) * 0.05
        ab = jax.random.normal(ks[5], (1,), dtype=jnp.float32) * 0.05
        Wk = jax.random.normal(ks[6], (K, DIN, DOUT), dtype=jnp.float32) * 0.02
        bk = jax.random.normal(ks[7], (K, DOUT), dtype=jnp.float32) * 0.02
        return {'X': X, 'A': A, 'Wv': Wv, 'bv': bv, 'aw': aw, 'ab': ab, 'Wk': Wk, 'bk': bk}
    _L0_gnn_all = _L0_gnn_setup()
    _L0_gnn_in = {k: v for k, v in _L0_gnn_all.items() if k in ('Wv', 'bv', 'aw', 'ab', 'Wk', 'bk')}
    del _L0_gnn_all

    def _L1_gnn_setup():
        import jax, jax.numpy as jnp
        import numpy as np
        EPS = 1e-06
        key = jax.random.key(seed)
        k1, k2, k3 = jax.random.split(key, 3)
        B, N, F, O = (8, 2048, 256, 256)
        x = jax.random.normal(k1, (B, N, F), dtype=jnp.float32)
        adj = jax.random.uniform(k2, (B, N, N), dtype=jnp.float32)
        W = jax.random.normal(k3, (O, 2 * F), dtype=jnp.float32) * (1.0 / np.sqrt(2 * F))
        return {'x': x, 'adj': adj, 'W': W}
    _L1_gnn_all = _L1_gnn_setup()
    _L1_gnn_in = {k: v for k, v in _L1_gnn_all.items() if k in ('W',)}
    del _L1_gnn_all

    def _L2_gnn_setup():
        import jax, jax.numpy as jnp
        import numpy as np
        N = 4096
        F = 256
        C = 256
        key = jax.random.key(seed)
        k1, k2, k3 = jax.random.split(key, 3)
        X = jax.random.normal(k1, (1, N, F), dtype=jnp.float32)
        A = jax.random.uniform(k2, (1, N, N), dtype=jnp.float32)
        kernel = jax.random.normal(k3, (F, C), dtype=jnp.float32) * (1.0 / np.sqrt(F))
        bias = jnp.zeros((C,), dtype=jnp.float32)
        return {'X': X, 'A': A, 'kernel': kernel, 'bias': bias}
    _L2_gnn_all = _L2_gnn_setup()
    _L2_gnn_in = {k: v for k, v in _L2_gnn_all.items() if k in ('kernel', 'bias')}
    del _L2_gnn_all

    def _L3_gnn_setup():
        import jax, jax.numpy as jnp
        import numpy as np
        B, N, D_IN, D_OUT = (4, 2048, 256, 256)
        key = jax.random.key(seed)
        k1, k2, k3, k4 = jax.random.split(key, 4)
        x = jax.random.normal(k1, (B, N, D_IN), dtype=jnp.float32)
        A_shape = jax.random.uniform(k2, (B, N, N), dtype=jnp.float32)
        w = jax.random.normal(k3, (D_IN, D_OUT), dtype=jnp.float32)
        a = jax.random.normal(k4, (D_OUT,), dtype=jnp.float32)
        return {'x': x, 'A_shape': A_shape, 'w': w, 'a': a}
    _L3_gnn_all = _L3_gnn_setup()
    _L3_gnn_in = {k: v for k, v in _L3_gnn_all.items() if k in ('w', 'a')}
    del _L3_gnn_all
    return {'x': x, 'adj': adj, 'L0_gnn_Wv': _L0_gnn_in['Wv'], 'L0_gnn_bv': _L0_gnn_in['bv'], 'L0_gnn_aw': _L0_gnn_in['aw'], 'L0_gnn_ab': _L0_gnn_in['ab'], 'L0_gnn_Wk': _L0_gnn_in['Wk'], 'L0_gnn_bk': _L0_gnn_in['bk'], 'L1_gnn_W': _L1_gnn_in['W'], 'L2_gnn_kernel': _L2_gnn_in['kernel'], 'L2_gnn_bias': _L2_gnn_in['bias'], 'L3_gnn_w': _L3_gnn_in['w'], 'L3_gnn_a': _L3_gnn_in['a']}

def reference(x, adj, L0_gnn_Wv, L0_gnn_bv, L0_gnn_aw, L0_gnn_ab, L0_gnn_Wk, L0_gnn_bk, L1_gnn_W, L2_gnn_kernel, L2_gnn_bias, L3_gnn_w, L3_gnn_a):
    import jax
    import jax.numpy as jnp

    def _L0_gnn_ref(X, A, Wv, bv, aw, ab, Wk, bk):
        import jax, jax.numpy as jnp
        import numpy as np
        B, N, DIN, DOUT, K = (4, 1024, 256, 256, 3)
        d = Wv.shape[1]
        Xw = X @ Wv + bv
        sj = Xw @ aw[:d, 0]
        si = Xw @ aw[d:, 0]
        e = jax.nn.leaky_relu(sj[:, None, :] + si[:, :, None] + ab[0], negative_slope=0.2)
        alpha_matrix = A * jnp.exp(e)
        transition = alpha_matrix / (jnp.sum(alpha_matrix, axis=-1, keepdims=True) + 1e-12)
        H = jnp.zeros(X.shape[:-1] + (d,), dtype=X.dtype)
        Xk = X
        for k in range(Wk.shape[0]):
            H = H + Xk @ Wk[k] + bk[k]
            Xk = jnp.einsum('bij,bjd->bid', transition, Xk)
        return jax.nn.relu(H)

    def _L1_gnn_ref(x, adj, W):
        import jax, jax.numpy as jnp
        import numpy as np
        EPS = 1e-06
        deg = jnp.sum(adj, axis=-1, keepdims=True)
        agg = jnp.einsum('bij,bjf->bif', adj, x) / jnp.maximum(deg, EPS)
        cat = jnp.concatenate([x, agg], axis=2)
        out = jnp.einsum('bnf,of->bno', cat, W)
        return jax.nn.relu(out)

    def _L2_gnn_ref(X, A, kernel, bias):
        import jax, jax.numpy as jnp
        import numpy as np
        N = 4096
        F = 256
        C = 256
        Ah = A + jnp.eye(A.shape[-1], dtype=A.dtype)[None, :, :]
        dh = jax.lax.rsqrt(jnp.sum(Ah, axis=-1))
        An = dh[:, :, None] * Ah * dh[:, None, :]
        out = jnp.einsum('bnm,bmf,fc->bnc', An, X, kernel) + bias
        return jax.nn.relu(out)

    def _L3_gnn_ref(x, A_shape, w, a):
        import jax, jax.numpy as jnp
        import numpy as np
        B, N, D_IN, D_OUT = (4, 2048, 256, 256)
        y = x @ w
        s = y @ a
        A = s[..., :, None] + s[..., None, :]
        A = jnp.tanh(A / 8.0) * 8.0
        A = jnp.where(A >= 0, A, 0.1 * A)
        A = jnp.exp(A) * A_shape
        A = A / jnp.sum(A, axis=-1, keepdims=True)
        A = A * jnp.sum(A_shape, axis=-1, keepdims=True)
        out = A @ x @ w
        return out
    h = jnp.maximum(_layernorm(x, axis=-1), 0.0)
    x = x + _L0_gnn_ref(h, adj, L0_gnn_Wv, L0_gnn_bv, L0_gnn_aw, L0_gnn_ab, L0_gnn_Wk, L0_gnn_bk)
    h = jnp.maximum(_layernorm(x, axis=-1), 0.0)
    x = x + _L1_gnn_ref(h, adj, L1_gnn_W)
    h = jnp.maximum(_layernorm(x, axis=-1), 0.0)
    x = x + _L2_gnn_ref(h, adj, L2_gnn_kernel, L2_gnn_bias)
    h = jnp.maximum(_layernorm(x, axis=-1), 0.0)
    x = x + _L3_gnn_ref(h, adj, L3_gnn_w, L3_gnn_a)
    return x

_drawn_inputs = setup_inputs


def setup_inputs(seed=0):
    import zlib

    import numpy as np

    out = dict(_drawn_inputs(seed))
    spreads = {'L2_gnn_bias': (0.0, 0.1)}
    factors = {'L0_gnn_Wv': 8.0, 'L0_gnn_bv': 36.236, 'L0_gnn_aw': 8.0}
    for name, (base, spread) in spreads.items():
        noise = np.random.default_rng([zlib.crc32(name.encode()), seed]).standard_normal(out[name].shape)
        drawn = base * np.exp(spread * noise) if base else spread * noise
        out[name] = jnp.asarray(drawn.astype(out[name].dtype))
    for name, factor in factors.items():
        out[name] = (out[name] * factor).astype(out[name].dtype)
    return out
```

```python
from contextlib import ExitStack

import concourse.bass as bass
from concourse import mybir

F32 = mybir.dt.float32
F32R = mybir.dt.float32r
ALU = mybir.AluOpType
ACT = mybir.ActivationFunctionType
AX = mybir.AxisListType

P = 128
G = 2
STAGES = 5
RING = 4
LN_EPS = 1e-5
SUM_EPS = 1e-12
DEG_EPS = 1e-6
W0, W1, W2, WSELF, WAGG, WGCN, WATT = range(7)


def graph_layers(nc, x, adj, wv_t, bv, aw, ab, wk, bk, w_cat_t, w_gcn, b_gcn, w_att, w_att_t, a_att, out):
    n_graphs, nodes, feat = x.shape
    pairs = n_graphs // G
    chunks = feat // P
    width = G * feat
    n_bk = wk.shape[0]
    assert nodes == P and width == 512 and pairs % RING == 0

    x_d = x.rearrange("(q b) n d -> q n b d", b=G)
    adj_d = adj.rearrange("(q b) i j -> q i b j", b=G)
    out_d = out.rearrange("(q b) n d -> q n b d", b=G)

    with ExitStack() as ctx:
        def sb(name, shape, dt=F32):
            return ctx.enter_context(nc.sbuf_tensor(name, shape, dt))

        def sem(name):
            return ctx.enter_context(nc.semaphore(name))

        ones = sb("ones", [P, P])
        ident = sb("ident", [P, P])
        minus_half = sb("minus_half", [P, G])
        minus_one = sb("minus_one", [P, G])
        ln_eps = sb("ln_eps", [P, G])
        wts = sb("wts", [P, 7, chunks, feat])
        wts_hi = sb("wts_hi", [P, 7, chunks, feat], F32R)
        wts_lo = sb("wts_lo", [P, 7, chunks, feat], F32R)
        wv_t_sb = sb("wv_t_sb", [P, chunks, feat])
        w_att_t_sb = sb("w_att_t_sb", [P, chunks, feat])
        aw_sb = sb("aw_sb", [P, chunks, 2])
        bv_sb = sb("bv_sb", [P, chunks])
        ab_sb = sb("ab_sb", [1, 1])
        a_att_sb = sb("a_att_sb", [P, chunks])
        u_hi = sb("u_hi", [P, chunks, 2], F32R)
        u_lo = sb("u_lo", [P, chunks, 2], F32R)
        score_const = sb("score_const", [P, G, 2])
        wa_row = sb("wa_row", [P, feat])
        bias_f32 = sb("bias_f32", [2 * n_bk, 2, feat])
        bias_hi = sb("bias_hi", [2 * n_bk, 2, feat], F32R)
        bias_lo = sb("bias_lo", [2 * n_bk, 2, feat], F32R)
        bias_l0 = sb("bias_l0", [2 * n_bk, feat], F32R)
        bias_l2 = sb("bias_l2", [2, feat], F32R)
        ones_r = sb("ones_r", [2 * n_bk, P], F32R)

        x0 = sb("x0", [P, RING, G, feat])
        x1 = sb("x1", [P, 2, G, feat])
        x2 = sb("x2", [P, 2, G, feat])
        x3 = sb("x3", [P, 2, G, feat])
        y = sb("y", [P, 2, G, feat])
        adj_sb = sb("adj_sb", [P, RING, G, P])

        stats = sb("stats", [P, STAGES, G, 6])
        moments = sb("moments", [P, STAGES, G, 2])
        var_eps = sb("var_eps", [P, STAGES, G])
        rstd = sb("rstd", [P, STAGES, G])
        neg_mean = sb("neg_mean", [P, STAGES, G])
        shift = sb("shift", [P, STAGES, G])
        gcn_scale = sb("gcn_scale", [P, G])
        gcn_shift = sb("gcn_shift", [P, G])
        h = sb("h", [P, STAGES, G, feat])

        h0t_hi = sb("h0t_hi", [P, 2, chunks, G, P], F32R)
        h0t_lo = sb("h0t_lo", [P, 2, chunks, G, P], F32R)
        s0 = sb("s0", [P, G, 2])
        z0 = sb("z0", [P, G, P])
        lz0 = sb("lz0", [P, G, P])
        e0 = sb("e0", [P, G, P])
        alpha0 = sb("alpha0", [P, G, P])
        row0 = sb("row0", [P, G])
        row0e = sb("row0e", [P, G])
        rrow0 = sb("rrow0", [P, G])
        trans = sb("trans", [P, 2, G, P])
        deg = sb("deg", [P, RING, G])
        deg_max = sb("deg_max", [P, G])
        rdeg = sb("rdeg", [P, G])
        deg_1 = sb("deg_1", [P, G])
        dh = sb("dh", [P, RING, G])
        adj_mean = sb("adj_mean", [P, G, P])
        adj_self = sb("adj_self", [P, G, P])
        adj_gcn = sb("adj_gcn", [P, G, P])
        adj_mean_t = sb("adj_mean_t", [P, RING, G, P])
        adj_gcn_t = sb("adj_gcn_t", [P, RING, G, P])
        trans_t = sb("trans_t", [P, G, P])
        hw2 = sb("hw2", [P, G, feat])
        inner = sb("inner", [P, G, feat])
        h2t_hi = sb("h2t_hi", [P, chunks, G, P], F32R)
        h2t_lo = sb("h2t_lo", [P, chunks, G, P], F32R)
        agg_hi = sb("agg_hi", [P, STAGES, chunks, G, P], F32R)
        agg_lo = sb("agg_lo", [P, STAGES, chunks, G, P], F32R)
        ttr_out = sb("ttr_out", [P, feat])
        s4 = sb("s4", [P, G])
        s4_8 = sb("s4_8", [P, G])
        th = sb("th", [P, G, P])
        lth = sb("lth", [P, G, P])
        e4 = sb("e4", [P, G, P])
        alpha4_t = sb("alpha4_t", [P, G, P])
        rrow4 = sb("rrow4", [P, G])
        scale4 = sb("scale4", [P, G])

        banks = ctx.enter_context(nc.psum_tensor("banks", [P, 8, width], F32))

        def cols(bank, inner_width):
            return banks[:, bank, 0:G * inner_width].rearrange("p (b d) -> p b d", b=G)

        hw2_ps, s0_ps = cols(0, feat), banks[:, 0, 0:4].rearrange("p (b k) -> p b k", b=G)
        inner_ps, row4_ps = cols(1, feat), banks[:, 1, 0:G]
        outer_ps = cols(2, feat)
        turn_ps = banks[:, 3, :].rearrange("p (c b n) -> p c b n", c=chunks, b=G)
        agg_ps = banks[:, 4, :].rearrange("p (c b n) -> p c b n", c=chunks, b=G)
        res_ps = cols(5, feat)
        pair_ps = cols(6, P)
        gcn_agg_ps = banks[:, 7, :].rearrange("p (c b n) -> p c b n", c=chunks, b=G)
        gcn_t_ps, gcn_ps = cols(7, P), cols(7, feat)

        x_landed = [sem(f"x_landed{r}") for r in range(RING)]
        adj_landed = [sem(f"adj_landed{r}") for r in range(RING)]
        y_stored = [sem(f"y_stored{r}") for r in range(2)]
        S = {name: sem(name) for name in (
            "w_landed", "small_landed", "bias_moved", "const_made", "setup_pe", "setup_dve",
            *[f"{e}{s}" for s in (0, 2, 3, 4) for e in ("stats_", "moments_", "vareps_", "rstd_", "negm_", "shift_", "h_")],
            "gcnscale_", "gcnshift_",
            "h0t_ps", "h0t_hi", "h0t_lo", "s0_ps", "s0_sb", "s0_row", "z0", "lz0", "e0", "alpha0", "row0e", "rrow0",
            "trans",
            "deg", "degmax", "deg1", "rdeg", "dh", "adj_mean", "adj_self", "adj_gcn",
            "adj_mean_t_ps", "adj_mean_t", "adj_gcn_t_ps", "adj_gcn_t", "trans_t_ps", "trans_t",
            "hw2_ps", "hw2", "inner_ps", "inner", "outer_ps", "x1",
            "h2t_ps", "h2t_hi", "h2t_lo", "agg2_ps", "agg2_hi", "agg2_lo", "res2_ps", "x2",
            "agg3_ps", "agg3_hi", "agg3_lo", "res3_ps", "x3",
            "s4", "s4_8", "s4_row", "th", "lth", "e4", "alpha4", "row4_ps", "rrow4", "scale4",
            "agg4_ps", "agg4_hi", "agg4_lo", "res4_ps", "y")}

        def steps(engine, step):
            for t in range(2 * RING):
                step(t // RING, t % RING, [0 <= t - s < pairs for s in range(STAGES)])
            with engine.Fori(2, pairs // RING) as q:
                for k in range(RING):
                    step(q, k, [True] * STAGES)
            for t in range(pairs, pairs + STAGES - 1):
                step(t // RING, t % RING, [0 <= t - s < pairs for s in range(STAGES)])

        def wait(engine, name, q, k, stage, back=0):
            count = RING * q + (k - stage - back + 1)
            if isinstance(count, int):
                count = min(count, pairs)
                if count <= 0:
                    return
            engine.wait_ge(S[name], count)

        def wait_slot(engine, slots, q, k, stage, ring, back=0):
            at = k - stage - back
            count = (RING // ring) * q + (at // ring + 1)
            if not isinstance(count, int) or count > 0:
                engine.wait_ge(slots[at % ring], 16 * count)

        def slot(k, stage, ring):
            return (k - stage) % ring

        block = ctx.enter_context(nc.Block())

        @block.sync
        def _(sp):
            smalls = [
                (wv_t_sb[:, :, :], wv_t.rearrange("(c p) d -> p c d", p=P)),
                (aw_sb[:, :, :], aw),
                (bv_sb[:, :], bv),
                (ab_sb[:, :], ab.rearrange("(a b) -> a b", a=1)),
                (w_att_t_sb[:, :, :], w_att_t.rearrange("(c p) d -> p c d", p=P)),
                (a_att_sb[:, :], a_att),
                (bias_f32[0:n_bk, 0, :], bk),
                (bias_f32[0:1, 1, :], b_gcn.rearrange("(a b) -> a b", a=1)),
            ]

            def load(q, k):
                r = slot(k, 0, RING)
                wait(sp, "x1", q, k, 0, back=RING)
                sp.dma_start(x0[:, r, :, :], x_d[RING * q + k]).then_inc(x_landed[r], 16)
                wait(sp, "adj_gcn", q, k, 0, back=RING)
                wait(sp, "adj_mean", q, k, 0, back=RING)
                sp.dma_start(adj_sb[:, r, :, :], adj_d[RING * q + k]).then_inc(adj_landed[r], 16)

            load(0, 0)
            for dst, src in smalls:
                sp.dma_start(dst, src).then_inc(S["small_landed"], 16)
            load(0, 1)
            sp.dma_start(wts[:, W0:W2 + 1, :, :].rearrange("p k c o -> p (k c) o"),
                         wk.rearrange("k (c p) o -> p (k c) o", p=P)).then_inc(S["w_landed"], 16)
            sp.dma_start(wts[:, WSELF:WAGG + 1, :, :].rearrange("p k c o -> p (k c) o"),
                         w_cat_t.rearrange("(k p) o -> p k o", p=P)).then_inc(S["w_landed"], 16)
            sp.dma_start(wts[:, WGCN, :, :], w_gcn.rearrange("(c p) o -> p c o", p=P)).then_inc(S["w_landed"], 16)
            sp.dma_start(wts[:, WATT, :, :], w_att.rearrange("(c p) o -> p c o", p=P)).then_inc(S["w_landed"], 16)
            sp.wait_ge(S["setup_dve"], 2)
            sp.dma_start(bias_l0[0:n_bk, :].bitcast(F32), bias_hi[0:n_bk, 0, :].bitcast(F32)).then_inc(S["bias_moved"], 16)
            sp.dma_start(bias_l0[n_bk:2 * n_bk, :].bitcast(F32), bias_lo[0:n_bk, 0, :].bitcast(F32)).then_inc(S["bias_moved"], 16)
            sp.dma_start(bias_l2[0:1, :].bitcast(F32), bias_hi[0:1, 1, :].bitcast(F32)).then_inc(S["bias_moved"], 16)
            sp.dma_start(bias_l2[1:2, :].bitcast(F32), bias_lo[0:1, 1, :].bitcast(F32)).then_inc(S["bias_moved"], 16)

            def step(q, k, on, ahead):
                if ahead:
                    load(q, k + 2)
                if on[4]:
                    r = slot(k, 4, 2)
                    wait(sp, "y", q, k, 4)
                    sp.dma_start(out_d[RING * q + (k - 4)], y[:, r, :, :]).then_inc(y_stored[r], 16)

            for t in range(2 * RING):
                q, k = divmod(t, RING)
                load(*divmod(t + 2, RING))
                step(q, k, [0 <= t - s < pairs for s in range(STAGES)], False)
            with sp.Fori(2, pairs // RING - 1) as q:
                for k in range(RING):
                    step(q, k, [True] * STAGES, True)
            for t in range(pairs - RING, pairs + STAGES - 1):
                q, k = divmod(t, RING)
                if t + 2 < pairs:
                    load(*divmod(t + 2, RING))
                step(q, k, [0 <= t - s < pairs for s in range(STAGES)], False)
            for r in range(2):
                sp.wait_ge(y_stored[r], 16 * (pairs // 2))

        @block.gpsimd
        def _(pool):
            pool.memset(ones[:, :], 1.0).then_inc(S["const_made"], 1)
            pool.memset(minus_half[:, :], -0.5).then_inc(S["const_made"], 1)
            pool.memset(minus_one[:, :], -1.0).then_inc(S["const_made"], 1)
            pool.memset(ln_eps[:, :], LN_EPS).then_inc(S["const_made"], 1)
            pool.memset(score_const[:, :, :], 0.0).then_inc(S["const_made"], 1)
            pool.wait_ge(S["const_made"], 5)
            pool.affine_select(out=ident[:, :], in_=ones[:, :], compare_op=ALU.is_equal, fill=0.0, base=0,
                               pattern=[[-1, P]], channel_multiplier=1).then_inc(S["const_made"], 1)
            pool.wait_ge(S["const_made"], 6)

            def per_row(v):
                return v.unsqueeze(2).to_broadcast([P, G, P])

            def norm(q, k, s):
                wait(pool, f"moments_{s}", q, k, s)
                wait(pool, f"h_{s}", q, k, s, back=1)
                pool.tensor_tensor(var_eps[:, s, :], moments[:, s, :, 1], ln_eps[:, :], ALU.add)\
                    .then_inc(S[f"vareps_{s}"], 1)
                pool.tensor_tensor(neg_mean[:, s, :], moments[:, s, :, 0], minus_one[:, :], ALU.mult)\
                    .then_inc(S[f"negm_{s}"], 1)
                wait(pool, f"vareps_{s}", q, k, s)
                pool.tensor_tensor(rstd[:, s, :], var_eps[:, s, :], minus_half[:, :], ALU.pow)\
                    .then_inc(S[f"rstd_{s}"], 1)
                wait(pool, f"negm_{s}", q, k, s)
                wait(pool, f"rstd_{s}", q, k, s)
                pool.tensor_tensor(shift[:, s, :], neg_mean[:, s, :], rstd[:, s, :], ALU.mult)\
                    .then_inc(S[f"shift_{s}"], 1)
                if s == 3:
                    r = slot(k, 3, RING)
                    wait(pool, "shift_3", q, k, s)
                    pool.tensor_tensor(gcn_scale[:, :], rstd[:, 3, :], dh[:, r, :], ALU.mult)\
                        .then_inc(S["gcnscale_"], 1)
                    pool.tensor_tensor(gcn_shift[:, :], shift[:, 3, :], dh[:, r, :], ALU.mult)\
                        .then_inc(S["gcnshift_"], 1)

            def step(q, k, on):
                if on[4]:
                    norm(q, k, 4)
                if on[2]:
                    norm(q, k, 2)
                if on[1]:
                    r = slot(k, 1, RING)
                    wait(pool, "deg", q, k, 1)
                    pool.tensor_tensor(deg_1[:, :], deg[:, r, :], ones[:, 0:G], ALU.add).then_inc(S["deg1"], 1)
                    wait(pool, "deg1", q, k, 1)
                    pool.tensor_tensor(dh[:, r, :], deg_1[:, :], minus_half[:, :], ALU.pow).then_inc(S["dh"], 1)
                    wait(pool, "adj_gcn_t_ps", q, k, 1, back=1)
                    pool.tensor_tensor(adj_self[:, :, :], adj_sb[:, r, :, :],
                                       ident[:, :].unsqueeze(1).to_broadcast([P, G, P]), ALU.add)\
                        .then_inc(S["adj_self"], 1)
                    wait(pool, "rdeg", q, k, 1)
                    wait(pool, "adj_mean_t_ps", q, k, 1, back=1)
                    pool.tensor_tensor(adj_mean[:, :, :], adj_sb[:, r, :, :], per_row(rdeg[:, :]), ALU.mult)\
                        .then_inc(S["adj_mean"], 1)
                    wait(pool, "dh", q, k, 1)
                    wait(pool, "adj_self", q, k, 1)
                    pool.tensor_tensor(adj_gcn[:, :, :], adj_self[:, :, :], per_row(dh[:, r, :]), ALU.mult)\
                        .then_inc(S["adj_gcn"], 1)
                if on[3]:
                    norm(q, k, 3)
                if on[0]:
                    norm(q, k, 0)
                    wait(pool, "rrow0", q, k, 0)
                    wait(pool, "trans_t_ps", q, k, 0, back=2)
                    pool.tensor_tensor(trans[:, slot(k, 0, 2), :, :], alpha0[:, :, :], per_row(rrow0[:, :]),
                                       ALU.mult).then_inc(S["trans"], 1)

            steps(pool, step)

        @block.scalar
        def _(act):
            def normalise(q, k, s):
                src, ring = {0: (x0, RING), 2: (x1, 2), 3: (x2, 2), 4: (x3, 2)}[s]
                scale, bias = (gcn_scale, gcn_shift) if s == 3 else (rstd[:, s, :], shift[:, s, :])
                wait(act, "gcnshift_" if s == 3 else f"shift_{s}", q, k, s)
                if s == 0:
                    wait(act, "h0t_ps", q, k, s, back=1)
                else:
                    wait(act, f"agg{s}_ps", q, k, s, back=1)
                if s == 2:
                    wait(act, "h2t_ps", q, k, s, back=1)
                if s == 4:
                    wait(act, "s4", q, k, s, back=1)
                for b in range(G):
                    last = act.activation(h[:, s, b, :], src[:, slot(k, s, ring), b, :], ACT.Relu,
                                          bias=bias[:, b:b + 1], scale=scale[:, b:b + 1])
                last.then_inc(S[f"h_{s}"], 1)

            def agg_hi_copy(q, k, s, ps):
                wait(act, f"agg{s}_ps", q, k, s)
                wait(act, f"res{s}_ps", q, k, s, back=1)
                act.copy(agg_hi[:, s, :, :, :], ps).then_inc(S[f"agg{s}_hi"], 1)

            def step(q, k, on):
                if on[4]:
                    normalise(q, k, 4)
                if on[1]:
                    wait(act, "hw2_ps", q, k, 1)
                    wait(act, "inner_ps", q, k, 1, back=1)
                    act.copy(hw2[:, :, :], hw2_ps).then_inc(S["hw2"], 1)
                if on[2]:
                    normalise(q, k, 2)
                if on[4]:
                    wait(act, "s4_row", q, k, 4)
                    wait(act, "s4_8", q, k, 4)
                    wait(act, "lth", q, k, 4, back=1)
                    for b in range(G):
                        last = act.activation(th[:, b, :], pair_ps[:, b, :], ACT.Tanh, bias=s4_8[:, b:b + 1],
                                              scale=0.125)
                    last.then_inc(S["th"], 1)
                if on[2]:
                    wait(act, "h2t_ps", q, k, 2)
                    wait(act, "res2_ps", q, k, 2, back=1)
                    act.copy(h2t_hi[:, :, :, :], turn_ps).then_inc(S["h2t_hi"], 1)
                    agg_hi_copy(q, k, 2, agg_ps)
                if on[3]:
                    normalise(q, k, 3)
                if on[4]:
                    wait(act, "lth", q, k, 4)
                    wait(act, "alpha4", q, k, 4, back=1)
                    act.activation(e4[:, :, :], lth[:, :, :], ACT.Exp, scale=8.0).then_inc(S["e4"], 1)
                if on[1]:
                    wait(act, "inner_ps", q, k, 1)
                    wait(act, "outer_ps", q, k, 1, back=1)
                    act.copy(inner[:, :, :], inner_ps).then_inc(S["inner"], 1)
                if on[0]:
                    normalise(q, k, 0)
                if on[3]:
                    agg_hi_copy(q, k, 3, gcn_agg_ps)
                if on[0]:
                    wait(act, "h0t_ps", q, k, 0)
                    wait(act, "outer_ps", q, k, 0, back=2)
                    act.copy(h0t_hi[:, slot(k, 0, 2), :, :, :], turn_ps).then_inc(S["h0t_hi"], 1)
                if on[4]:
                    agg_hi_copy(q, k, 4, agg_ps)
                if on[0]:
                    wait(act, "s0_row", q, k, 0)
                    wait(act, "lz0", q, k, 0, back=1)
                    for b in range(G):
                        last = act.activation(z0[:, b, :], pair_ps[:, b, :], ACT.Identity, bias=s0[:, b, 1:2])
                    last.then_inc(S["z0"], 1)
                    wait(act, "lz0", q, k, 0)
                    wait(act, "alpha0", q, k, 0, back=1)
                    act.activation(e0[:, :, :], lz0[:, :, :], ACT.Exp).then_inc(S["e0"], 1)

            steps(act, step)

        @block.vector
        def _(dve):
            dve.wait_ge(S["small_landed"], 16 * 8)
            dve.tensor_copy(bias_hi[0:n_bk, 0, :], bias_f32[0:n_bk, 0, :])
            dve.tensor_copy(bias_hi[0:1, 1, :], bias_f32[0:1, 1, :]).then_inc(S["setup_dve"], 1)
            dve.wait_ge(S["setup_dve"], 1)
            dve.tensor_tensor(bias_lo[0:n_bk, 0, :], bias_f32[0:n_bk, 0, :],
                              bias_hi[0:n_bk, 0, :].bitcast(F32), ALU.subtract)
            dve.tensor_tensor(bias_lo[0:1, 1, :], bias_f32[0:1, 1, :],
                              bias_hi[0:1, 1, :].bitcast(F32), ALU.subtract).then_inc(S["setup_dve"], 1)
            dve.wait_ge(S["setup_pe"], 1)
            dve.wait_ge(S["const_made"], 6)
            u_ps = banks[:, 0, 0:2 * chunks].rearrange("p (c k) -> p c k", c=chunks)
            dve.tensor_copy(u_hi[:, :, :], u_ps)
            dve.tensor_copy(score_const[:, 0, 1:2], banks[:, 1, 0:1])
            dve.tensor_copy(score_const[:, 1, 1:2], banks[:, 1, 0:1])
            dve.tensor_copy(wa_row[:, :], banks[:, 2, 0:feat])
            dve.tensor_copy(ones_r[:, :], ones[0:2 * n_bk, :]).then_inc(S["setup_dve"], 1)
            dve.wait_ge(S["setup_dve"], 3)
            dve.tensor_tensor(u_lo[:, :, :], u_ps, u_hi[:, :, :].bitcast(F32), ALU.subtract)\
                .then_inc(S["setup_dve"], 1)
            dve.wait_ge(S["w_landed"], 16 * 4)
            dve.tensor_copy(wts_hi[:, :, :, :], wts[:, :, :, :]).then_inc(S["setup_dve"], 1)
            dve.wait_ge(S["setup_dve"], 5)
            dve.tensor_tensor(wts_lo[:, :, :, :], wts[:, :, :, :], wts_hi[:, :, :, :].bitcast(F32), ALU.subtract)\
                .then_inc(S["setup_dve"], 1)

            def stats_of(q, k, s):
                src, ring = {0: (x0, RING), 2: (x1, 2), 3: (x2, 2), 4: (x3, 2)}[s]
                if s == 0:
                    wait_slot(dve, x_landed, q, k, 0, RING)
                else:
                    wait(dve, f"x{s - 1}", q, k, s)
                wait(dve, f"moments_{s}", q, k, s, back=1)
                for b in range(G):
                    last = dve.bn_stats(stats[:, s, b, :], src[:, slot(k, s, ring), b, :])
                last.then_inc(S[f"stats_{s}"], 1)

            def wait_moments(q, k, s):
                wait(dve, f"stats_{s}", q, k, s)
                wait(dve, f"negm_{s}", q, k, s, back=1)
                wait(dve, f"vareps_{s}", q, k, s, back=1)

            def moments_of(q, k, s):
                for b in range(G):
                    last = dve.bn_aggr(moments[:, s, b, :], stats[:, s, b, :])
                last.then_inc(S[f"moments_{s}"], 1)

            def agg_lo_sub(q, k, s, ps):
                wait(dve, f"agg{s}_hi", q, k, s)
                wait(dve, f"res{s}_ps", q, k, s, back=1)
                dve.tensor_tensor(agg_lo[:, s, :, :, :], ps, agg_hi[:, s, :, :, :].bitcast(F32), ALU.subtract)\
                    .then_inc(S[f"agg{s}_lo"], 1)

            def residual(q, k, s, ps, src, src_ring, dst, name):
                wait(dve, {1: "outer_ps", 2: "res2_ps", 3: "res3_ps"}[s], q, k, s)
                wait(dve, f"h_{s + 1}", q, k, s, back=2)
                wait(dve, name, q, k, s, back=1)
                dve.scalar_tensor_tensor(out=dst[:, slot(k, s, 2), :, :], in0=ps, scalar=0.0,
                                         in1=src[:, slot(k, s, src_ring), :, :], op0=ALU.max, op1=ALU.add)\
                    .then_inc(S[name], 1)

            def step(q, k, on):
                if on[4]:
                    stats_of(q, k, 4)
                    wait_moments(q, k, 4)
                if on[2]:
                    stats_of(q, k, 2)
                if on[4]:
                    moments_of(q, k, 4)
                if on[2]:
                    wait_moments(q, k, 2)
                if on[1]:
                    r = slot(k, 1, RING)
                    wait(dve, "trans_t_ps", q, k, 1)
                    wait(dve, "outer_ps", q, k, 1, back=1)
                    dve.tensor_copy(trans_t[:, :, :], pair_ps).then_inc(S["trans_t"], 1)
                if on[2]:
                    moments_of(q, k, 2)
                if on[1]:
                    wait_slot(dve, adj_landed, q, k, 1, RING)
                    dve.tensor_reduce(deg[:, r, :], adj_sb[:, r, :, :], AX.X, ALU.add).then_inc(S["deg"], 1)
                if on[4]:
                    wait(dve, "h_4", q, k, 4)
                    wait(dve, "s4_row", q, k, 4, back=1)
                    for b in range(G):
                        if b:
                            dve.wait_ge(S["s4"], 2 * RING * q + 2 * (k - 4) + 1)
                        elif not isinstance(q, int) or RING * q + k > 4:
                            dve.wait_ge(S["s4"], 2 * RING * q + 2 * (k - 4))
                        dve.tensor_tensor_reduce(ttr_out[:, :], h[:, 4, b, :], wa_row[:, :], 1.0, 0.0,
                                                 ALU.mult, ALU.add, s4[:, b:b + 1]).then_inc(S["s4"], 1)
                    dve.wait_ge(S["s4"], 2 * RING * q + 2 * (k - 4) + 2)
                    wait(dve, "th", q, k, 4, back=1)
                    dve.tensor_scalar(s4_8[:, :], s4[:, :], 0.125, None, ALU.mult).then_inc(S["s4_8"], 1)
                if on[1]:
                    wait(dve, "deg", q, k, 1)
                    dve.tensor_scalar(deg_max[:, :], deg[:, slot(k, 1, RING), :], DEG_EPS, None, ALU.max)\
                        .then_inc(S["degmax"], 1)
                    wait(dve, "degmax", q, k, 1)
                    wait(dve, "adj_mean", q, k, 1, back=1)
                    dve.reciprocal(rdeg[:, :], deg_max[:, :]).then_inc(S["rdeg"], 1)
                if on[3]:
                    stats_of(q, k, 3)
                    wait_moments(q, k, 3)
                if on[0]:
                    stats_of(q, k, 0)
                if on[3]:
                    moments_of(q, k, 3)
                if on[0]:
                    wait_moments(q, k, 0)
                if on[2]:
                    wait(dve, "h2t_hi", q, k, 2)
                    wait(dve, "res2_ps", q, k, 2, back=1)
                    dve.tensor_tensor(h2t_lo[:, :, :, :], turn_ps, h2t_hi[:, :, :, :].bitcast(F32), ALU.subtract)\
                        .then_inc(S["h2t_lo"], 1)
                if on[0]:
                    moments_of(q, k, 0)
                if on[2]:
                    agg_lo_sub(q, k, 2, agg_ps)
                if on[4]:
                    wait(dve, "th", q, k, 4)
                    wait(dve, "e4", q, k, 4, back=1)
                    dve.scalar_tensor_tensor(out=lth[:, :, :], in0=th[:, :, :], scalar=0.1, in1=th[:, :, :],
                                             op0=ALU.mult, op1=ALU.max).then_inc(S["lth"], 1)
                if on[1]:
                    wait(dve, "adj_mean_t_ps", q, k, 1)
                    wait(dve, "agg4_ps", q, k, 1, back=RING)
                    dve.tensor_copy(adj_mean_t[:, slot(k, 1, RING), :, :], pair_ps).then_inc(S["adj_mean_t"], 1)
                if on[3]:
                    agg_lo_sub(q, k, 3, gcn_agg_ps)
                if on[2]:
                    residual(q, k, 2, res_ps, x1, 2, x2, "x2")
                if on[4]:
                    wait(dve, "e4", q, k, 4)
                    wait(dve, "agg4_ps", q, k, 4, back=1)
                    dve.tensor_tensor(alpha4_t[:, :, :], e4[:, :, :], adj_mean_t[:, slot(k, 4, RING), :, :],
                                      ALU.mult).then_inc(S["alpha4"], 1)
                if on[1]:
                    residual(q, k, 1, outer_ps, x0, RING, x1, "x1")
                if on[0]:
                    wait(dve, "h0t_hi", q, k, 0)
                    wait(dve, "outer_ps", q, k, 0, back=2)
                    dve.tensor_tensor(h0t_lo[:, slot(k, 0, 2), :, :, :], turn_ps,
                                      h0t_hi[:, slot(k, 0, 2), :, :, :].bitcast(F32), ALU.subtract)\
                        .then_inc(S["h0t_lo"], 1)
                if on[1]:
                    wait(dve, "adj_gcn_t_ps", q, k, 1)
                    wait(dve, "agg3_ps", q, k, 1, back=RING)
                    dve.tensor_copy(adj_gcn_t[:, slot(k, 1, RING), :, :], gcn_t_ps).then_inc(S["adj_gcn_t"], 1)
                if on[0]:
                    wait(dve, "s0_ps", q, k, 0)
                    wait(dve, "s0_row", q, k, 0, back=1)
                    wait(dve, "z0", q, k, 0, back=1)
                    dve.tensor_tensor(s0[:, :, :], s0_ps, score_const[:, :, :], ALU.add).then_inc(S["s0_sb"], 1)
                if on[4]:
                    agg_lo_sub(q, k, 4, agg_ps)
                    r = slot(k, 4, RING)
                    wait(dve, "row4_ps", q, k, 4)
                    dve.reciprocal(rrow4[:, :], row4_ps).then_inc(S["rrow4"], 1)
                    wait(dve, "rrow4", q, k, 4)
                    dve.tensor_tensor(scale4[:, :], rrow4[:, :], deg[:, r, :], ALU.mult).then_inc(S["scale4"], 1)
                if on[0]:
                    wait(dve, "z0", q, k, 0)
                    wait(dve, "e0", q, k, 0, back=1)
                    dve.scalar_tensor_tensor(out=lz0[:, :, :], in0=z0[:, :, :], scalar=0.2, in1=z0[:, :, :],
                                             op0=ALU.mult, op1=ALU.max).then_inc(S["lz0"], 1)
                if on[3]:
                    residual(q, k, 3, gcn_ps, x2, 2, x3, "x3")
                if on[0]:
                    wait(dve, "e0", q, k, 0)
                    wait_slot(dve, adj_landed, q, k, 0, RING)
                    wait(dve, "trans", q, k, 0, back=1)
                    wait(dve, "row0e", q, k, 0, back=1)
                    for b in range(G):
                        last = dve.tensor_tensor_reduce(alpha0[:, b, :], e0[:, b, :],
                                                        adj_sb[:, slot(k, 0, RING), b, :], 1.0, 0.0,
                                                        ALU.mult, ALU.add, row0[:, b:b + 1])
                    last.then_inc(S["alpha0"], 1)
                    wait(dve, "alpha0", q, k, 0)
                    dve.tensor_scalar(row0e[:, :], row0[:, :], SUM_EPS, None, ALU.add).then_inc(S["row0e"], 1)
                    wait(dve, "row0e", q, k, 0)
                    dve.reciprocal(rrow0[:, :], row0e[:, :]).then_inc(S["rrow0"], 1)
                if on[4]:
                    ry = slot(k, 4, 2)
                    wait(dve, "res4_ps", q, k, 4)
                    wait(dve, "scale4", q, k, 4)
                    wait_slot(dve, y_stored, q, k, 4, 2, back=2)
                    for b in range(G):
                        last = dve.scalar_tensor_tensor(out=y[:, ry, b, :], in0=res_ps[:, b, :],
                                                        scalar=scale4[:, b:b + 1], in1=x3[:, slot(k, 4, 2), b, :],
                                                        op0=ALU.mult, op1=ALU.add)
                    last.then_inc(S["y"], 1)

            steps(dve, step)

        @block.tensor
        def _(pe):
            pe.wait_ge(S["small_landed"], 16 * 8)
            pe.wait_ge(S["const_made"], 6)
            for c in range(chunks):
                for o in range(chunks):
                    pe.matmul(banks[:, 0, 2 * c:2 * c + 2], wv_t_sb[:, o, c * P:(c + 1) * P], aw_sb[:, o, :],
                              start=(c == 0 and o == 0), stop=(o == chunks - 1), skip_group_check=True)
            for o in range(chunks):
                for j in range(2):
                    pe.matmul(banks[:, 1, 0:1], bv_sb[:, o:o + 1].to_broadcast([P, P]), aw_sb[:, o, j:j + 1],
                              start=(o == 0 and j == 0), stop=False)
            pe.matmul(banks[:, 1, 0:1], ones[0:1, :], ab_sb[:, :], start=False, stop=True)
            for o in range(chunks):
                last = pe.matmul(banks[:, 2, 0:feat], a_att_sb[:, o:o + 1].to_broadcast([P, P]), w_att_t_sb[:, o, :],
                                 start=(o == 0), stop=(o == chunks - 1))
            last.then_inc(S["setup_pe"], 1)
            pe.wait_ge(S["setup_dve"], 6)
            pe.wait_ge(S["bias_moved"], 16 * 4)

            def weigh(dst, hi, lo, w, first, closes=True):
                for b in range(G):
                    for c in range(chunks):
                        for i, (left, right) in enumerate(((hi, wts_hi), (hi, wts_lo), (lo, wts_hi))):
                            last = pe.matmul(dst[:, b, :], left[:, c, b, :], right[:, w, c, :],
                                             start=(first and b == 0 and c == 0 and i == 0),
                                             stop=(closes and c == chunks - 1 and i == 2), skip_group_check=True)
                return last

            def turn_h(s):
                for c in range(chunks):
                    for b in range(G):
                        last = pe.transpose(turn_ps[:, c, b, :], h[:, s, b, c * P:(c + 1) * P], ident[:, :])
                return last

            def aggregate(dst, s, mat):
                for c in range(chunks):
                    for b in range(G):
                        last = pe.matmul(dst[:, c, b, :], h[:, s, b, c * P:(c + 1) * P], mat[:, b, :],
                                         start=True, stop=True)
                return last

            def step(q, k, on):
                if on[1]:
                    r = slot(k, 1, 2)
                    wait(pe, "trans", q, k, 1)
                    wait(pe, "z0", q, k, 0, back=1)
                    for b in range(G):
                        last = pe.transpose(pair_ps[:, b, :], trans[:, r, b, :], ident[:, :])
                    last.then_inc(S["trans_t_ps"], 1)
                    wait(pe, "h0t_lo", q, k, 1)
                    wait(pe, "h0t_hi", q, k, 1)
                    wait(pe, "s0_sb", q, k, 1)
                    weigh(hw2_ps, h0t_hi[:, r], h0t_lo[:, r], W2, True).then_inc(S["hw2_ps"], 1)
                    wait(pe, "rrow4", q, k, 4, back=1)
                    weigh(inner_ps, h0t_hi[:, r], h0t_lo[:, r], W1, True, False)
                    wait(pe, "x1", q, k, 1, back=1)
                    pe.matmul(outer_ps, ones_r[:, :],
                              bias_l0[:, :].unsqueeze(1).to_broadcast([2 * n_bk, G, feat]), start=True, stop=False,
                              skip_group_check=True)
                    weigh(outer_ps, h0t_hi[:, r], h0t_lo[:, r], W0, False, False)
                if on[2]:
                    wait(pe, "h_2", q, k, 2)
                    wait(pe, "h0t_lo", q, k, 0, back=1)
                    turn_h(2).then_inc(S["h2t_ps"], 1)
                    wait(pe, "agg4_lo", q, k, 4, back=1)
                    aggregate(agg_ps, 2, adj_mean_t[:, slot(k, 2, RING)]).then_inc(S["agg2_ps"], 1)
                if on[4]:
                    wait(pe, "s4_8", q, k, 4)
                    if on[1]:
                        wait(pe, "trans_t", q, k, 1)
                    else:
                        wait(pe, "z0", q, k, 0, back=1)
                    for b in range(G):
                        last = pe.transpose(pair_ps[:, b, :], s4[:, b:b + 1].to_broadcast([P, P]), ident[:, :])
                    last.then_inc(S["s4_row"], 1)
                if on[1]:
                    wait(pe, "hw2", q, k, 1)
                    wait(pe, "trans_t", q, k, 1)
                    for b in range(G):
                        last = pe.matmul(inner_ps[:, b, :], trans_t[:, b, :], hw2[:, b, :], start=False, stop=True,
                                         skip_group_check=True)
                    last.then_inc(S["inner_ps"], 1)
                if on[3]:
                    wait(pe, "h_3", q, k, 3)
                    wait(pe, "x3", q, k, 3, back=1)
                    aggregate(gcn_agg_ps, 3, adj_gcn_t[:, slot(k, 3, RING)]).then_inc(S["agg3_ps"], 1)
                if on[2]:
                    wait(pe, "h2t_lo", q, k, 2)
                    wait(pe, "y", q, k, 4, back=1)
                    weigh(res_ps, h2t_hi, h2t_lo, WSELF, True, False)
                    wait(pe, "agg2_lo", q, k, 2)
                    weigh(res_ps, agg_hi[:, 2], agg_lo[:, 2], WAGG, False).then_inc(S["res2_ps"], 1)
                if on[1]:
                    if on[4]:
                        wait(pe, "th", q, k, 4)
                    wait(pe, "adj_mean", q, k, 1)
                    for b in range(G):
                        last = pe.transpose(pair_ps[:, b, :], adj_mean[:, b, :], ident[:, :])
                    last.then_inc(S["adj_mean_t_ps"], 1)
                    wait(pe, "inner", q, k, 1)
                    for b in range(G):
                        last = pe.matmul(outer_ps[:, b, :], trans_t[:, b, :], inner[:, b, :], start=False, stop=True,
                                         skip_group_check=True)
                    last.then_inc(S["outer_ps"], 1)
                if on[0]:
                    wait(pe, "h_0", q, k, 0)
                    if on[2]:
                        wait(pe, "h2t_lo", q, k, 2)
                    turn_h(0).then_inc(S["h0t_ps"], 1)
                if on[4]:
                    wait(pe, "alpha4", q, k, 4)
                    if on[2]:
                        wait(pe, "agg2_lo", q, k, 2)
                    aggregate(agg_ps, 4, alpha4_t).then_inc(S["agg4_ps"], 1)
                    if on[1]:
                        wait(pe, "inner", q, k, 1)
                    for b in range(G):
                        last = pe.matmul(row4_ps[:, b:b + 1], alpha4_t[:, b, :], ones[:, 0:1], start=True, stop=True)
                    last.then_inc(S["row4_ps"], 1)
                if on[1]:
                    wait(pe, "adj_gcn", q, k, 1)
                    if on[3]:
                        wait(pe, "agg3_lo", q, k, 3)
                    for b in range(G):
                        last = pe.transpose(gcn_t_ps[:, b, :], adj_gcn[:, b, :], ident[:, :])
                    last.then_inc(S["adj_gcn_t_ps"], 1)
                if on[0]:
                    r = slot(k, 0, 2)
                    wait(pe, "h0t_lo", q, k, 0)
                    if on[1]:
                        wait(pe, "hw2", q, k, 1)
                    for b in range(G):
                        for c in range(chunks):
                            for i, (left, right) in enumerate(((h0t_hi, u_hi), (h0t_hi, u_lo), (h0t_lo, u_hi))):
                                last = pe.matmul(s0_ps[:, b, :], left[:, r, c, b, :], right[:, c, :],
                                                 start=(c == 0 and i == 0), stop=(c == chunks - 1 and i == 2))
                    last.then_inc(S["s0_ps"], 1)
                if on[3]:
                    if on[1]:
                        wait(pe, "adj_gcn_t", q, k, 1)
                    wait(pe, "agg3_lo", q, k, 3)
                    pe.matmul(gcn_ps, ones_r[0:2, :], bias_l2[:, :].unsqueeze(1).to_broadcast([2, G, feat]),
                              start=True, stop=False, skip_group_check=True)
                    weigh(gcn_ps, agg_hi[:, 3], agg_lo[:, 3], WGCN, False).then_inc(S["res3_ps"], 1)
                if on[0]:
                    wait(pe, "s0_sb", q, k, 0)
                    if on[1]:
                        wait(pe, "adj_mean_t", q, k, 1)
                    for b in range(G):
                        last = pe.transpose(pair_ps[:, b, :], s0[:, b, 0:1].to_broadcast([P, P]), ident[:, :])
                    last.then_inc(S["s0_row"], 1)
                if on[4]:
                    wait(pe, "agg4_lo", q, k, 4)
                    if on[2]:
                        wait(pe, "x2", q, k, 2)
                    weigh(res_ps, agg_hi[:, 4], agg_lo[:, 4], WATT, True).then_inc(S["res4_ps"], 1)

            steps(pe, step)


def kernel(x, adj, L0_gnn_Wv, L0_gnn_bv, L0_gnn_aw, L0_gnn_ab, L0_gnn_Wk, L0_gnn_bk, L1_gnn_W, L2_gnn_kernel,
           L2_gnn_bias, L3_gnn_w, L3_gnn_a):
    import numpy as _np
    import concourse.bacc as _bacc
    from concourse import mybir as _mybir
    from concourse.bass_utils import run_bass_kernel_spmd as _run

    nc = _bacc.Bacc("TRN2", target_bir_lowering=False, num_devices=1)
    chunks = x.shape[2] // P
    aw_rows = _np.asarray(L0_gnn_aw).reshape(2, chunks, P).transpose(2, 1, 0)
    bv_rows = _np.asarray(L0_gnn_bv).reshape(chunks, P).T
    a_rows = _np.asarray(L3_gnn_a).reshape(chunks, P).T
    laid_out = {
        "x": x, "adj": adj, "wv_t": L0_gnn_Wv.T, "bv": bv_rows, "aw": aw_rows, "ab": L0_gnn_ab,
        "wk": L0_gnn_Wk, "bk": L0_gnn_bk, "w_cat_t": L1_gnn_W.T, "w_gcn": L2_gnn_kernel, "b_gcn": L2_gnn_bias,
        "w_att": L3_gnn_w, "w_att_t": L3_gnn_w.T, "a_att": a_rows,
    }
    arrays, args = {}, []
    for name, a in laid_out.items():
        a = _np.ascontiguousarray(a)
        arrays[f"in_{name}"] = a
        args.append(nc.dram_tensor(f"in_{name}", a.shape, _mybir.dt.from_np(a.dtype), kind="ExternalInput").ap())
    args.append(nc.dram_tensor("out", x.shape, _mybir.dt.float32, kind="ExternalOutput").ap())
    graph_layers(nc, *args)
    r = _run(nc, [arrays], core_ids=[0])
    return r.results[0]["out"]
```

```python
from contextlib import ExitStack

import concourse.bass as bass
from concourse import mybir

F32 = mybir.dt.float32
F32R = mybir.dt.float32r
ALU = mybir.AluOpType
ACT = mybir.ActivationFunctionType
AX = mybir.AxisListType

P = 128
G = 2
STAGES = 5
RING = 4
LN_EPS = 1e-5
SUM_EPS = 1e-12
DEG_EPS = 1e-6
W0, W1, W2, WSELF, WAGG, WGCN, WATT = range(7)


def graph_layers(nc, x, adj, wv_t, bv, aw, ab, wk, bk, w_cat_t, w_gcn, b_gcn, w_att, w_att_t, a_att, out):
    n_graphs, nodes, feat = x.shape
    pairs = n_graphs // G
    chunks = feat // P
    width = G * feat
    n_bk = wk.shape[0]
    assert nodes == P and width == 512 and pairs % RING == 0

    x_d = x.rearrange("(q b) n d -> q n b d", b=G)
    adj_d = adj.rearrange("(q b) i j -> q i b j", b=G)
    out_d = out.rearrange("(q b) n d -> q n b d", b=G)

    with ExitStack() as ctx:
        def sb(name, shape, dt=F32):
            return ctx.enter_context(nc.sbuf_tensor(name, shape, dt))

        def sem(name):
            return ctx.enter_context(nc.semaphore(name))

        ones = sb("ones", [P, P])
        ident = sb("ident", [P, P])
        minus_half = sb("minus_half", [P, G])
        minus_one = sb("minus_one", [P, G])
        ln_eps = sb("ln_eps", [P, G])
        wts = sb("wts", [P, 7, chunks, feat])
        wts_hi = sb("wts_hi", [P, 7, chunks, feat], F32R)
        wts_lo = sb("wts_lo", [P, 7, chunks, feat], F32R)
        wv_t_sb = sb("wv_t_sb", [P, chunks, feat])
        w_att_t_sb = sb("w_att_t_sb", [P, chunks, feat])
        aw_sb = sb("aw_sb", [P, chunks, 2])
        bv_sb = sb("bv_sb", [P, chunks])
        ab_sb = sb("ab_sb", [1, 1])
        a_att_sb = sb("a_att_sb", [P, chunks])
        u = sb("u", [P, chunks, 4], F32R)
        score_const = sb("score_const", [P, G, 2])
        wa_row = sb("wa_row", [P, feat])
        bias_f32 = sb("bias_f32", [2 * n_bk, 2, feat])
        bias_hi = sb("bias_hi", [2 * n_bk, 2, feat], F32R)
        bias_lo = sb("bias_lo", [2 * n_bk, 2, feat], F32R)
        bias_l0 = sb("bias_l0", [2 * n_bk, feat], F32R)
        bias_l2 = sb("bias_l2", [2, feat], F32R)
        ones_r = sb("ones_r", [2 * n_bk, P], F32R)

        x0 = sb("x0", [P, RING, G, feat])
        x1 = sb("x1", [P, 2, G, feat])
        x2 = sb("x2", [P, 2, G, feat])
        x3 = sb("x3", [P, 2, G, feat])
        y = sb("y", [P, 2, G, feat])
        adj_sb = sb("adj_sb", [P, RING, G, P])

        stats = sb("stats", [P, STAGES, G, 6])
        moments = sb("moments", [P, STAGES, G, 2])
        var_eps = sb("var_eps", [P, STAGES, G])
        rstd = sb("rstd", [P, STAGES, G])
        neg_mean = sb("neg_mean", [P, STAGES, G])
        shift = sb("shift", [P, STAGES, G])
        gcn_scale = sb("gcn_scale", [P, G])
        gcn_shift = sb("gcn_shift", [P, G])
        h = sb("h", [P, STAGES, G, feat])

        h0t_hi = sb("h0t_hi", [P, 2, chunks, G, P], F32R)
        h0t_lo = sb("h0t_lo", [P, 2, chunks, G, P], F32R)
        s0_part = sb("s0_part", [P, G, 2])
        s0 = sb("s0", [P, G, 2])
        z0 = sb("z0", [P, G, P])
        lz0 = sb("lz0", [P, G, P])
        e0 = sb("e0", [P, G, P])
        alpha0 = sb("alpha0", [P, G, P])
        row0 = sb("row0", [P, G])
        row0e = sb("row0e", [P, G])
        rrow0 = sb("rrow0", [P, G])
        trans = sb("trans", [P, 2, G, P])
        deg = sb("deg", [P, RING, G])
        deg_max = sb("deg_max", [P, G])
        rdeg = sb("rdeg", [P, G])
        deg_1 = sb("deg_1", [P, G])
        dh = sb("dh", [P, RING, G])
        adj_mean = sb("adj_mean", [P, G, P])
        adj_self = sb("adj_self", [P, G, P])
        adj_gcn = sb("adj_gcn", [P, G, P])
        adj_mean_t = sb("adj_mean_t", [P, RING, G, P])
        adj_gcn_t = sb("adj_gcn_t", [P, RING, G, P])
        trans_t = sb("trans_t", [P, G, P])
        hw2 = sb("hw2", [P, G, feat])
        inner = sb("inner", [P, G, feat])
        h2t_hi = sb("h2t_hi", [P, chunks, G, P], F32R)
        h2t_lo = sb("h2t_lo", [P, chunks, G, P], F32R)
        agg_hi = sb("agg_hi", [P, STAGES, chunks, G, P], F32R)
        agg_lo = sb("agg_lo", [P, STAGES, chunks, G, P], F32R)
        ttr_out = sb("ttr_out", [P, G, feat])
        s4 = sb("s4", [P, G])
        s4_8 = sb("s4_8", [P, G])
        th = sb("th", [P, G, P])
        lth = sb("lth", [P, G, P])
        e4 = sb("e4", [P, G, P])
        alpha4_t = sb("alpha4_t", [P, G, P])
        rrow4 = sb("rrow4", [P, G])
        scale4 = sb("scale4", [P, G])

        banks = ctx.enter_context(nc.psum_tensor("banks", [P, 8, width], F32))

        def cols(bank, inner_width):
            return banks[:, bank, 0:G * inner_width].rearrange("p (b d) -> p b d", b=G)

        hw2_ps, s0_ps = cols(0, feat), banks[:, 0, 0:4 * G].rearrange("p (b k) -> p b k", b=G)
        inner_ps, row4_ps = cols(1, feat), banks[:, 1, 0:G]
        outer_ps = cols(2, feat)
        turn_ps = banks[:, 3, :].rearrange("p (c b n) -> p c b n", c=chunks, b=G)
        agg_ps = banks[:, 4, :].rearrange("p (c b n) -> p c b n", c=chunks, b=G)
        res_ps = cols(5, feat)
        pair_ps = cols(6, P)
        gcn_agg_ps = banks[:, 7, :].rearrange("p (c b n) -> p c b n", c=chunks, b=G)
        gcn_t_ps, gcn_ps = cols(7, P), cols(7, feat)

        x_landed = [sem(f"x_landed{r}") for r in range(RING)]
        adj_landed = [sem(f"adj_landed{r}") for r in range(RING)]
        y_stored = [sem(f"y_stored{r}") for r in range(2)]
        S = {name: sem(name) for name in (
            "w_landed", "small_landed", "bias_moved", "const_made", "setup_pe", "setup_dve",
            *[f"{e}{s}" for s in (0, 2, 3, 4) for e in ("stats_", "moments_", "vareps_", "rstd_", "negm_", "shift_", "h_")],
            "gcnscale_", "gcnshift_",
            "h0t_ps", "h0t_hi", "h0t_lo", "s0_ps", "s0_part", "s0_sb", "s0_row", "z0", "lz0", "e0", "alpha0", "row0e", "rrow0",
            "trans",
            "deg", "degmax", "deg1", "rdeg", "dh", "adj_mean", "adj_self", "adj_gcn",
            "adj_mean_t_ps", "adj_mean_t", "adj_gcn_t_ps", "adj_gcn_t", "trans_t_ps", "trans_t",
            "hw2_ps", "hw2", "inner_ps", "inner", "outer_ps", "x1",
            "h2t_ps", "h2t_hi", "h2t_lo", "agg2_ps", "agg2_hi", "agg2_lo", "res2_ps", "x2",
            "agg3_ps", "agg3_hi", "agg3_lo", "res3_ps", "x3",
            "s4", "s4_8", "s4_row", "th", "lth", "e4", "alpha4", "row4_ps", "rrow4", "scale4",
            "agg4_ps", "agg4_hi", "agg4_lo", "res4_ps", "y")}

        def steps(engine, step):
            def written_out(first, end):
                for t in range(first, end):
                    step(t // RING, t % RING, {s: 0 <= t - s < pairs for s in range(-1, STAGES)})

            written_out(-1, 2 * RING)
            with engine.Fori(2, pairs // RING - 1) as q:
                for k in range(RING):
                    step(q, k, {s: True for s in range(-1, STAGES)})
            written_out(pairs - RING, pairs + STAGES - 1)

        def wait(engine, name, q, k, stage, back=0):
            count = RING * q + (k - stage - back + 1)
            if isinstance(count, int):
                count = min(count, pairs)
                if count <= 0:
                    return
            engine.wait_ge(S[name], count)

        def wait_slot(engine, slots, q, k, stage, ring, back=0):
            at = k - stage - back
            count = (RING // ring) * q + (at // ring + 1)
            if not isinstance(count, int) or count > 0:
                engine.wait_ge(slots[at % ring], 16 * count)

        def slot(k, stage, ring):
            return (k - stage) % ring

        block = ctx.enter_context(nc.Block())

        @block.sync
        def _(sp):
            smalls = [
                (wv_t_sb[:, :, :], wv_t.rearrange("(c p) d -> p c d", p=P)),
                (aw_sb[:, :, :], aw),
                (bv_sb[:, :], bv),
                (ab_sb[:, :], ab.rearrange("(a b) -> a b", a=1)),
                (w_att_t_sb[:, :, :], w_att_t.rearrange("(c p) d -> p c d", p=P)),
                (a_att_sb[:, :], a_att),
                (bias_f32[0:n_bk, 0, :], bk),
                (bias_f32[0:1, 1, :], b_gcn.rearrange("(a b) -> a b", a=1)),
            ]

            def load(q, k):
                r = slot(k, 0, RING)
                wait(sp, "x1", q, k, 0, back=RING)
                sp.dma_start(x0[:, r, :, :], x_d[RING * q + k]).then_inc(x_landed[r], 16)
                wait(sp, "adj_gcn", q, k, 0, back=RING)
                wait(sp, "adj_mean", q, k, 0, back=RING)
                sp.dma_start(adj_sb[:, r, :, :], adj_d[RING * q + k]).then_inc(adj_landed[r], 16)

            load(0, 0)
            for dst, src in smalls:
                sp.dma_start(dst, src).then_inc(S["small_landed"], 16)
            load(0, 1)
            sp.dma_start(wts[:, W0:W2 + 1, :, :].rearrange("p k c o -> p (k c) o"),
                         wk.rearrange("k (c p) o -> p (k c) o", p=P)).then_inc(S["w_landed"], 16)
            sp.dma_start(wts[:, WSELF:WAGG + 1, :, :].rearrange("p k c o -> p (k c) o"),
                         w_cat_t.rearrange("(k p) o -> p k o", p=P)).then_inc(S["w_landed"], 16)
            sp.dma_start(wts[:, WGCN, :, :], w_gcn.rearrange("(c p) o -> p c o", p=P)).then_inc(S["w_landed"], 16)
            sp.dma_start(wts[:, WATT, :, :], w_att.rearrange("(c p) o -> p c o", p=P)).then_inc(S["w_landed"], 16)
            sp.wait_ge(S["setup_dve"], 2)
            sp.dma_start(bias_l0[0:n_bk, :].bitcast(F32), bias_hi[0:n_bk, 0, :].bitcast(F32)).then_inc(S["bias_moved"], 16)
            sp.dma_start(bias_l0[n_bk:2 * n_bk, :].bitcast(F32), bias_lo[0:n_bk, 0, :].bitcast(F32)).then_inc(S["bias_moved"], 16)
            sp.dma_start(bias_l2[0:1, :].bitcast(F32), bias_hi[0:1, 1, :].bitcast(F32)).then_inc(S["bias_moved"], 16)
            sp.dma_start(bias_l2[1:2, :].bitcast(F32), bias_lo[0:1, 1, :].bitcast(F32)).then_inc(S["bias_moved"], 16)

            def step(q, k, on):
                if not isinstance(q, int) or 0 <= RING * q + k + 3 < pairs:
                    load(q, k + 3)
                if on[4]:
                    r = slot(k, 4, 2)
                    wait(sp, "y", q, k, 4)
                    sp.dma_start(out_d[RING * q + (k - 4)], y[:, r, :, :]).then_inc(y_stored[r], 16)

            steps(sp, step)
            for r in range(2):
                sp.wait_ge(y_stored[r], 16 * (pairs // 2))

        @block.gpsimd
        def _(pool):
            pool.memset(ones[:, :], 1.0).then_inc(S["const_made"], 1)
            pool.memset(minus_half[:, :], -0.5).then_inc(S["const_made"], 1)
            pool.memset(minus_one[:, :], -1.0).then_inc(S["const_made"], 1)
            pool.memset(ln_eps[:, :], LN_EPS).then_inc(S["const_made"], 1)
            pool.memset(score_const[:, :, :], 0.0).then_inc(S["const_made"], 1)
            pool.wait_ge(S["const_made"], 5)
            pool.affine_select(out=ident[:, :], in_=ones[:, :], compare_op=ALU.is_equal, fill=0.0, base=0,
                               pattern=[[-1, P]], channel_multiplier=1).then_inc(S["const_made"], 1)
            pool.wait_ge(S["const_made"], 6)

            def per_row(v):
                return v.unsqueeze(2).to_broadcast([P, G, P])

            def norm(q, k, s, at):
                wait(pool, f"moments_{s}", q, k, at)
                wait(pool, f"h_{s}", q, k, at, back=1)
                pool.tensor_tensor(var_eps[:, s, :], moments[:, s, :, 1], ln_eps[:, :], ALU.add)\
                    .then_inc(S[f"vareps_{s}"], 1)
                pool.tensor_tensor(neg_mean[:, s, :], moments[:, s, :, 0], minus_one[:, :], ALU.mult)\
                    .then_inc(S[f"negm_{s}"], 1)
                wait(pool, f"vareps_{s}", q, k, at)
                pool.tensor_tensor(rstd[:, s, :], var_eps[:, s, :], minus_half[:, :], ALU.pow)\
                    .then_inc(S[f"rstd_{s}"], 1)
                wait(pool, f"negm_{s}", q, k, at)
                wait(pool, f"rstd_{s}", q, k, at)
                pool.tensor_tensor(shift[:, s, :], neg_mean[:, s, :], rstd[:, s, :], ALU.mult)\
                    .then_inc(S[f"shift_{s}"], 1)
                if s == 3:
                    r = slot(k, at, RING)
                    wait(pool, "shift_3", q, k, at)
                    pool.tensor_tensor(gcn_scale[:, :], rstd[:, 3, :], dh[:, r, :], ALU.mult)\
                        .then_inc(S["gcnscale_"], 1)
                    pool.tensor_tensor(gcn_shift[:, :], shift[:, 3, :], dh[:, r, :], ALU.mult)\
                        .then_inc(S["gcnshift_"], 1)

            def step(q, k, on):
                if on[1]:
                    r = slot(k, 1, RING)
                    wait(pool, "deg", q, k, 1)
                    pool.tensor_tensor(deg_1[:, :], deg[:, r, :], ones[:, 0:G], ALU.add).then_inc(S["deg1"], 1)
                    wait(pool, "deg1", q, k, 1)
                    pool.tensor_tensor(dh[:, r, :], deg_1[:, :], minus_half[:, :], ALU.pow).then_inc(S["dh"], 1)
                    wait(pool, "adj_gcn_t_ps", q, k, 1, back=1)
                    pool.tensor_tensor(adj_self[:, :, :], adj_sb[:, r, :, :],
                                       ident[:, :].unsqueeze(1).to_broadcast([P, G, P]), ALU.add)\
                        .then_inc(S["adj_self"], 1)
                    wait(pool, "rdeg", q, k, 1)
                    wait(pool, "adj_mean_t_ps", q, k, 1, back=1)
                    pool.tensor_tensor(adj_mean[:, :, :], adj_sb[:, r, :, :], per_row(rdeg[:, :]), ALU.mult)\
                        .then_inc(S["adj_mean"], 1)
                    wait(pool, "dh", q, k, 1)
                    wait(pool, "adj_self", q, k, 1)
                    pool.tensor_tensor(adj_gcn[:, :, :], adj_self[:, :, :], per_row(dh[:, r, :]), ALU.mult)\
                        .then_inc(S["adj_gcn"], 1)
                if on[-1]:
                    norm(q, k, 0, -1)
                if on[0]:
                    wait(pool, "rrow0", q, k, 0)
                    wait(pool, "trans_t_ps", q, k, 0, back=2)
                    pool.tensor_tensor(trans[:, slot(k, 0, 2), :, :], alpha0[:, :, :], per_row(rrow0[:, :]),
                                       ALU.mult).then_inc(S["trans"], 1)
                if on[1]:
                    norm(q, k, 2, 1)
                if on[2]:
                    norm(q, k, 3, 2)
                if on[3]:
                    norm(q, k, 4, 3)

            steps(pool, step)

        @block.scalar
        def _(act):
            def normalise(q, k, s, at):
                src, ring = {0: (x0, RING), 2: (x1, 2), 3: (x2, 2), 4: (x3, 2)}[s]
                scale, bias = (gcn_scale, gcn_shift) if s == 3 else (rstd[:, s, :], shift[:, s, :])
                wait(act, "gcnshift_" if s == 3 else f"shift_{s}", q, k, at)
                if s in (0, 2):
                    wait(act, f"h{s}t_ps", q, k, at, back=1)
                if s > 0:
                    wait(act, f"agg{s}_ps", q, k, at, back=1)
                if s == 4:
                    wait(act, "s4", q, k, at, back=1)
                for b in range(G):
                    last = act.activation(h[:, s, b, :], src[:, slot(k, at, ring), b, :], ACT.Relu,
                                          bias=bias[:, b:b + 1], scale=scale[:, b:b + 1])
                last.then_inc(S[f"h_{s}"], 1)

            def agg_hi_copy(q, k, s, ps):
                wait(act, f"agg{s}_ps", q, k, s)
                wait(act, f"res{s}_ps", q, k, s, back=1)
                act.copy(agg_hi[:, s, :, :, :], ps).then_inc(S[f"agg{s}_hi"], 1)

            def step(q, k, on):
                if on[1]:
                    wait(act, "trans_t_ps", q, k, 1)
                    wait(act, "outer_ps", q, k, 1, back=1)
                    act.copy(trans_t[:, :, :], pair_ps).then_inc(S["trans_t"], 1)
                if on[0]:
                    wait(act, "h0t_ps", q, k, 0)
                    wait(act, "outer_ps", q, k, 0, back=2)
                    act.copy(h0t_hi[:, slot(k, 0, 2), :, :, :], turn_ps).then_inc(S["h0t_hi"], 1)
                if on[1]:
                    wait(act, "hw2_ps", q, k, 1)
                    wait(act, "inner_ps", q, k, 1, back=1)
                    act.copy(hw2[:, :, :], hw2_ps).then_inc(S["hw2"], 1)
                if on[2]:
                    wait(act, "h2t_ps", q, k, 2)
                    wait(act, "res2_ps", q, k, 2, back=1)
                    act.copy(h2t_hi[:, :, :, :], turn_ps).then_inc(S["h2t_hi"], 1)
                if on[4]:
                    normalise(q, k, 4, 4)
                if on[3]:
                    normalise(q, k, 3, 3)
                if on[2]:
                    agg_hi_copy(q, k, 2, agg_ps)
                if on[1]:
                    wait(act, "inner_ps", q, k, 1)
                    wait(act, "outer_ps", q, k, 1, back=1)
                    act.copy(inner[:, :, :], inner_ps).then_inc(S["inner"], 1)
                if on[4]:
                    wait(act, "s4_row", q, k, 4)
                    wait(act, "s4_8", q, k, 4)
                    wait(act, "lth", q, k, 4, back=1)
                    for b in range(G):
                        last = act.activation(th[:, b, :], pair_ps[:, b, :], ACT.Tanh, bias=s4_8[:, b:b + 1],
                                              scale=0.125)
                    last.then_inc(S["th"], 1)
                if on[-1]:
                    normalise(q, k, 0, -1)
                if on[4]:
                    wait(act, "lth", q, k, 4)
                    wait(act, "alpha4", q, k, 4, back=1)
                    act.activation(e4[:, :, :], lth[:, :, :], ACT.Exp, scale=8.0).then_inc(S["e4"], 1)
                if on[3]:
                    agg_hi_copy(q, k, 3, gcn_agg_ps)
                if on[0]:
                    wait(act, "s0_row", q, k, 0)
                    wait(act, "lz0", q, k, 0, back=1)
                    for b in range(G):
                        last = act.activation(z0[:, b, :], pair_ps[:, b, :], ACT.Identity, bias=s0[:, b, 1:2])
                    last.then_inc(S["z0"], 1)
                    wait(act, "lz0", q, k, 0)
                    wait(act, "alpha0", q, k, 0, back=1)
                    act.activation(e0[:, :, :], lz0[:, :, :], ACT.Exp).then_inc(S["e0"], 1)
                if on[4]:
                    agg_hi_copy(q, k, 4, agg_ps)
                if on[1]:
                    normalise(q, k, 2, 1)
                    wait(act, "adj_mean_t_ps", q, k, 1)
                    wait(act, "agg2_ps", q, k, 1, back=RING)
                    wait(act, "alpha4", q, k, 1, back=RING)
                    act.copy(adj_mean_t[:, slot(k, 1, RING), :, :], pair_ps).then_inc(S["adj_mean_t"], 1)
                if on[1]:
                    wait(act, "adj_gcn_t_ps", q, k, 1)
                    wait(act, "agg3_ps", q, k, 1, back=RING)
                    act.copy(adj_gcn_t[:, slot(k, 1, RING), :, :], gcn_t_ps).then_inc(S["adj_gcn_t"], 1)

            steps(act, step)

        @block.vector
        def _(dve):
            dve.wait_ge(S["small_landed"], 16 * 8)
            dve.tensor_copy(bias_hi[0:n_bk, 0, :], bias_f32[0:n_bk, 0, :])
            dve.tensor_copy(bias_hi[0:1, 1, :], bias_f32[0:1, 1, :]).then_inc(S["setup_dve"], 1)
            dve.wait_ge(S["setup_dve"], 1)
            dve.tensor_tensor(bias_lo[0:n_bk, 0, :], bias_f32[0:n_bk, 0, :],
                              bias_hi[0:n_bk, 0, :].bitcast(F32), ALU.subtract)
            dve.tensor_tensor(bias_lo[0:1, 1, :], bias_f32[0:1, 1, :],
                              bias_hi[0:1, 1, :].bitcast(F32), ALU.subtract).then_inc(S["setup_dve"], 1)
            dve.wait_ge(S["setup_pe"], 1)
            dve.wait_ge(S["const_made"], 6)
            u_ps = banks[:, 0, 0:2 * chunks].rearrange("p (c k) -> p c k", c=chunks)
            dve.tensor_copy(u[:, :, 0:2], u_ps)
            dve.tensor_copy(score_const[:, 0, 1:2], banks[:, 1, 0:1])
            dve.tensor_copy(score_const[:, 1, 1:2], banks[:, 1, 0:1])
            dve.tensor_copy(wa_row[:, :], banks[:, 2, 0:feat])
            dve.tensor_copy(ones_r[:, :], ones[0:2 * n_bk, :]).then_inc(S["setup_dve"], 1)
            dve.wait_ge(S["setup_dve"], 3)
            dve.tensor_tensor(u[:, :, 2:4], u_ps, u[:, :, 0:2].bitcast(F32), ALU.subtract)\
                .then_inc(S["setup_dve"], 1)
            dve.wait_ge(S["w_landed"], 16 * 4)
            dve.tensor_copy(wts_hi[:, :, :, :], wts[:, :, :, :]).then_inc(S["setup_dve"], 1)
            dve.wait_ge(S["setup_dve"], 5)
            dve.tensor_tensor(wts_lo[:, :, :, :], wts[:, :, :, :], wts_hi[:, :, :, :].bitcast(F32), ALU.subtract)\
                .then_inc(S["setup_dve"], 1)

            def stats_of(q, k, s, at):
                src, ring = {0: (x0, RING), 2: (x1, 2), 3: (x2, 2), 4: (x3, 2)}[s]
                wait(dve, f"moments_{s}", q, k, at, back=1)
                if s == 0:
                    wait_slot(dve, x_landed, q, k, at, RING)
                else:
                    wait(dve, f"x{s - 1}", q, k, at)
                for b in range(G):
                    last = dve.bn_stats(stats[:, s, b, :], src[:, slot(k, at, ring), b, :])
                last.then_inc(S[f"stats_{s}"], 1)

            def wait_moments(q, k, s, at):
                wait(dve, f"negm_{s}", q, k, at, back=1)
                wait(dve, f"vareps_{s}", q, k, at, back=1)
                wait(dve, f"stats_{s}", q, k, at)

            def moments_of(s):
                for b in range(G):
                    last = dve.bn_aggr(moments[:, s, b, :], stats[:, s, b, :])
                last.then_inc(S[f"moments_{s}"], 1)

            def agg_lo_sub(q, k, s, ps):
                wait(dve, f"agg{s}_hi", q, k, s)
                wait(dve, f"res{s}_ps", q, k, s, back=1)
                dve.tensor_tensor(agg_lo[:, s, :, :, :], ps, agg_hi[:, s, :, :, :].bitcast(F32), ALU.subtract)\
                    .then_inc(S[f"agg{s}_lo"], 1)

            def residual(q, k, s, ps, src, src_ring, dst, name):
                wait(dve, f"h_{s + 1}", q, k, s, back=2)
                wait(dve, {1: "outer_ps", 2: "res2_ps", 3: "res3_ps"}[s], q, k, s)
                dve.scalar_tensor_tensor(out=dst[:, slot(k, s, 2), :, :], in0=ps, scalar=0.0,
                                         in1=src[:, slot(k, s, src_ring), :, :], op0=ALU.max, op1=ALU.add)\
                    .then_inc(S[name], 1)

            def result(q, k, b):
                return dve.scalar_tensor_tensor(out=y[:, slot(k, 4, 2), b, :], in0=res_ps[:, b, :],
                                                scalar=scale4[:, b:b + 1], in1=x3[:, slot(k, 4, 2), b, :],
                                                op0=ALU.mult, op1=ALU.add)

            def step(q, k, on):
                if on[0]:
                    wait(dve, "outer_ps", q, k, 0, back=2)
                    wait(dve, "h0t_hi", q, k, 0)
                    dve.tensor_tensor(h0t_lo[:, slot(k, 0, 2), :, :, :], turn_ps,
                                      h0t_hi[:, slot(k, 0, 2), :, :, :].bitcast(F32), ALU.subtract)\
                        .then_inc(S["h0t_lo"], 1)
                if on[1]:
                    wait_slot(dve, adj_landed, q, k, 1, RING)
                    dve.tensor_reduce(deg[:, slot(k, 1, RING), :], adj_sb[:, slot(k, 1, RING), :, :], AX.X, ALU.add)\
                        .then_inc(S["deg"], 1)
                if on[-1]:
                    stats_of(q, k, 0, -1)
                    wait_moments(q, k, 0, -1)
                if on[1]:
                    wait(dve, "deg", q, k, 1)
                    dve.tensor_scalar(deg_max[:, :], deg[:, slot(k, 1, RING), :], DEG_EPS, None, ALU.max)\
                        .then_inc(S["degmax"], 1)
                if on[-1]:
                    moments_of(0)
                if on[1]:
                    wait(dve, "adj_mean", q, k, 1, back=1)
                    wait(dve, "degmax", q, k, 1)
                    dve.reciprocal(rdeg[:, :], deg_max[:, :]).then_inc(S["rdeg"], 1)
                if on[2]:
                    wait(dve, "res2_ps", q, k, 2, back=1)
                    wait(dve, "h2t_hi", q, k, 2)
                    dve.tensor_tensor(h2t_lo[:, :, :, :], turn_ps, h2t_hi[:, :, :, :].bitcast(F32), ALU.subtract)\
                        .then_inc(S["h2t_lo"], 1)
                if on[4]:
                    wait(dve, "s4_row", q, k, 4, back=1)
                    wait(dve, "h_4", q, k, 4)
                    for b in range(G):
                        last = dve.tensor_tensor_reduce(ttr_out[:, b, :], h[:, 4, b, :], wa_row[:, :], 1.0, 0.0,
                                                        ALU.mult, ALU.add, s4[:, b:b + 1])
                    last.then_inc(S["s4"], 1)
                    wait(dve, "th", q, k, 4, back=1)
                    wait(dve, "s4", q, k, 4)
                    dve.tensor_scalar(s4_8[:, :], s4[:, :], 0.125, None, ALU.mult).then_inc(S["s4_8"], 1)
                if on[2]:
                    agg_lo_sub(q, k, 2, agg_ps)
                if on[4]:
                    wait(dve, "e4", q, k, 4, back=1)
                    wait(dve, "th", q, k, 4)
                    dve.scalar_tensor_tensor(out=lth[:, :, :], in0=th[:, :, :], scalar=0.1, in1=th[:, :, :],
                                             op0=ALU.mult, op1=ALU.max).then_inc(S["lth"], 1)
                if on[0]:
                    wait(dve, "s0_ps", q, k, 0)
                    dve.tensor_tensor(s0_part[:, :, :], s0_ps[:, :, 2:4], score_const[:, :, :], ALU.add)\
                        .then_inc(S["s0_part"], 1)
                    wait(dve, "z0", q, k, 0, back=1)
                    wait(dve, "s0_row", q, k, 0, back=1)
                    wait(dve, "s0_part", q, k, 0)
                    dve.tensor_tensor(s0[:, :, :], s0_ps[:, :, 0:2], s0_part[:, :, :], ALU.add)\
                        .then_inc(S["s0_sb"], 1)
                if on[4]:
                    wait(dve, "agg4_ps", q, k, 4, back=1)
                    wait(dve, "row4_ps", q, k, 4, back=1)
                    wait(dve, "adj_mean_t", q, k, 4)
                    wait(dve, "e4", q, k, 4)
                    dve.tensor_tensor(alpha4_t[:, :, :], e4[:, :, :], adj_mean_t[:, slot(k, 4, RING), :, :],
                                      ALU.mult).then_inc(S["alpha4"], 1)
                if on[3]:
                    agg_lo_sub(q, k, 3, gcn_agg_ps)
                if on[0]:
                    wait(dve, "e0", q, k, 0, back=1)
                    wait(dve, "z0", q, k, 0)
                    dve.scalar_tensor_tensor(out=lz0[:, :, :], in0=z0[:, :, :], scalar=0.2, in1=z0[:, :, :],
                                             op0=ALU.mult, op1=ALU.max).then_inc(S["lz0"], 1)
                if on[1]:
                    residual(q, k, 1, outer_ps, x0, RING, x1, "x1")
                if on[0]:
                    wait(dve, "trans", q, k, 0, back=1)
                    wait(dve, "row0e", q, k, 0, back=1)
                    wait_slot(dve, adj_landed, q, k, 0, RING)
                    wait(dve, "e0", q, k, 0)
                    for b in range(G):
                        last = dve.tensor_tensor_reduce(alpha0[:, b, :], e0[:, b, :],
                                                        adj_sb[:, slot(k, 0, RING), b, :], 1.0, 0.0,
                                                        ALU.mult, ALU.add, row0[:, b:b + 1])
                    last.then_inc(S["alpha0"], 1)
                if on[1]:
                    stats_of(q, k, 2, 1)
                    wait_moments(q, k, 2, 1)
                if on[0]:
                    wait(dve, "alpha0", q, k, 0)
                    dve.tensor_scalar(row0e[:, :], row0[:, :], SUM_EPS, None, ALU.add).then_inc(S["row0e"], 1)
                if on[1]:
                    moments_of(2)
                if on[0]:
                    wait(dve, "row0e", q, k, 0)
                    dve.reciprocal(rrow0[:, :], row0e[:, :]).then_inc(S["rrow0"], 1)
                if on[4]:
                    wait(dve, "row4_ps", q, k, 4)
                    dve.reciprocal(rrow4[:, :], row4_ps).then_inc(S["rrow4"], 1)
                    agg_lo_sub(q, k, 4, agg_ps)
                    wait(dve, "rrow4", q, k, 4)
                    dve.tensor_tensor(scale4[:, :], rrow4[:, :], deg[:, slot(k, 4, RING), :], ALU.mult)\
                        .then_inc(S["scale4"], 1)
                if on[2]:
                    residual(q, k, 2, res_ps, x1, 2, x2, "x2")
                    stats_of(q, k, 3, 2)
                    wait_moments(q, k, 3, 2)
                if on[3]:
                    residual(q, k, 3, gcn_ps, x2, 2, x3, "x3")
                if on[2]:
                    moments_of(3)
                if on[3]:
                    stats_of(q, k, 4, 3)
                    wait_moments(q, k, 4, 3)
                if on[4]:
                    wait(dve, "scale4", q, k, 4)
                    wait_slot(dve, y_stored, q, k, 4, 2, back=2)
                    wait(dve, "res4_ps", q, k, 4)
                    result(q, k, 0)
                if on[3]:
                    moments_of(4)
                if on[4]:
                    result(q, k, 1).then_inc(S["y"], 1)

            steps(dve, step)

        @block.tensor
        def _(pe):
            pe.wait_ge(S["small_landed"], 16 * 8)
            pe.wait_ge(S["const_made"], 6)
            for c in range(chunks):
                for o in range(chunks):
                    pe.matmul(banks[:, 0, 2 * c:2 * c + 2], wv_t_sb[:, o, c * P:(c + 1) * P], aw_sb[:, o, :],
                              start=(c == 0 and o == 0), stop=(o == chunks - 1), skip_group_check=True)
            for o in range(chunks):
                for j in range(2):
                    pe.matmul(banks[:, 1, 0:1], bv_sb[:, o:o + 1].to_broadcast([P, P]), aw_sb[:, o, j:j + 1],
                              start=(o == 0 and j == 0), stop=False)
            pe.matmul(banks[:, 1, 0:1], ones[0:1, :], ab_sb[:, :], start=False, stop=True)
            for o in range(chunks):
                last = pe.matmul(banks[:, 2, 0:feat], a_att_sb[:, o:o + 1].to_broadcast([P, P]), w_att_t_sb[:, o, :],
                                 start=(o == 0), stop=(o == chunks - 1))
            last.then_inc(S["setup_pe"], 1)
            pe.wait_ge(S["setup_dve"], 6)
            pe.wait_ge(S["bias_moved"], 16 * 4)

            def weigh(dst, hi, lo, w, first, closes=True):
                for b in range(G):
                    for c in range(chunks):
                        for i, (left, right) in enumerate(((hi, wts_hi), (hi, wts_lo), (lo, wts_hi))):
                            last = pe.matmul(dst[:, b, :], left[:, c, b, :], right[:, w, c, :],
                                             start=(first and b == 0 and c == 0 and i == 0),
                                             stop=(closes and c == chunks - 1 and i == 2), skip_group_check=True)
                return last

            def turn_h(s):
                for c in range(chunks):
                    for b in range(G):
                        last = pe.transpose(turn_ps[:, c, b, :], h[:, s, b, c * P:(c + 1) * P], ident[:, :])
                return last

            def aggregate(dst, s, mat):
                for c in range(chunks):
                    for b in range(G):
                        last = pe.matmul(dst[:, c, b, :], h[:, s, b, c * P:(c + 1) * P], mat[:, b, :],
                                         start=True, stop=True)
                return last

            def turn_pair(src):
                for b in range(G):
                    last = pe.transpose(pair_ps[:, b, :], src(b), ident[:, :])
                return last

            def step(q, k, on):
                r0, r1 = slot(k, 0, 2), slot(k, 1, 2)
                if on[1]:
                    wait(pe, "adj_mean_t", q, k, 1, back=1)
                    wait(pe, "trans", q, k, 1)
                    turn_pair(lambda b: trans[:, r1, b, :]).then_inc(S["trans_t_ps"], 1)
                if on[0]:
                    wait(pe, "h2t_lo", q, k, 2, back=1)
                    wait(pe, "h_0", q, k, 0)
                    turn_h(0).then_inc(S["h0t_ps"], 1)
                if on[1]:
                    wait(pe, "s0_sb", q, k, 1)
                    wait(pe, "h0t_hi", q, k, 1)
                    wait(pe, "h0t_lo", q, k, 1)
                    weigh(hw2_ps, h0t_hi[:, r1], h0t_lo[:, r1], W2, True).then_inc(S["hw2_ps"], 1)
                if on[1]:
                    wait(pe, "rrow4", q, k, 4, back=1)
                    weigh(inner_ps, h0t_hi[:, r1], h0t_lo[:, r1], W1, True, False)
                if on[2]:
                    wait(pe, "h_2", q, k, 2)
                    if on[0]:
                        wait(pe, "h0t_lo", q, k, 0)
                    else:
                        wait(pe, "h0t_lo", q, k, 0, back=1)
                    turn_h(2).then_inc(S["h2t_ps"], 1)
                if on[2]:
                    wait(pe, "adj_mean_t", q, k, 2)
                    wait(pe, "agg4_lo", q, k, 4, back=1)
                    aggregate(agg_ps, 2, adj_mean_t[:, slot(k, 2, RING)]).then_inc(S["agg2_ps"], 1)
                if on[1]:
                    wait(pe, "trans_t", q, k, 1)
                    wait(pe, "hw2", q, k, 1)
                    for b in range(G):
                        last = pe.matmul(inner_ps[:, b, :], trans_t[:, b, :], hw2[:, b, :], start=False, stop=True,
                                         skip_group_check=True)
                    last.then_inc(S["inner_ps"], 1)
                if on[0]:
                    if on[1]:
                        wait(pe, "hw2", q, k, 1)
                    wait(pe, "h0t_hi", q, k, 0)
                    wait(pe, "h0t_lo", q, k, 0)
                    for b in range(G):
                        for c in range(chunks):
                            pe.matmul(s0_ps[:, b, :], h0t_hi[:, r0, c, b, :], u[:, c, :], start=(c == 0), stop=False,
                                      skip_group_check=True)
                            last = pe.matmul(s0_ps[:, b, 0:2], h0t_lo[:, r0, c, b, :], u[:, c, 0:2], start=False,
                                             stop=(c == chunks - 1), skip_group_check=True)
                    last.then_inc(S["s0_ps"], 1)
                if on[4]:
                    if not on[1]:
                        wait(pe, "adj_mean_t", q, k, 1, back=1)
                        wait(pe, "z0", q, k, 0, back=1)
                    wait(pe, "s4", q, k, 4)
                    turn_pair(lambda b: s4[:, b:b + 1].to_broadcast([P, P])).then_inc(S["s4_row"], 1)
                if on[1]:
                    wait(pe, "x1", q, k, 1, back=1)
                    pe.matmul(outer_ps, ones_r[:, :],
                              bias_l0[:, :].unsqueeze(1).to_broadcast([2 * n_bk, G, feat]), start=True, stop=False,
                              skip_group_check=True)
                    weigh(outer_ps, h0t_hi[:, r1], h0t_lo[:, r1], W0, False, False)
                if on[3]:
                    wait(pe, "h_3", q, k, 3)
                    wait(pe, "adj_gcn_t", q, k, 2)
                    aggregate(gcn_agg_ps, 3, adj_gcn_t[:, slot(k, 3, RING)]).then_inc(S["agg3_ps"], 1)
                if on[0]:
                    wait(pe, "s0_sb", q, k, 0)
                    if on[1]:
                        wait(pe, "trans_t", q, k, 1)
                    if on[4]:
                        wait(pe, "th", q, k, 4)
                    turn_pair(lambda b: s0[:, b, 0:1].to_broadcast([P, P])).then_inc(S["s0_row"], 1)
                if on[1]:
                    wait(pe, "inner", q, k, 1)
                    for b in range(G):
                        last = pe.matmul(outer_ps[:, b, :], trans_t[:, b, :], inner[:, b, :], start=False, stop=True,
                                         skip_group_check=True)
                    last.then_inc(S["outer_ps"], 1)
                if on[4]:
                    if on[2]:
                        wait(pe, "agg2_lo", q, k, 2)
                    else:
                        wait(pe, "agg4_lo", q, k, 4, back=1)
                    wait(pe, "alpha4", q, k, 4)
                    aggregate(agg_ps, 4, alpha4_t).then_inc(S["agg4_ps"], 1)
                    wait(pe, "rrow4", q, k, 4, back=1)
                    for b in range(G):
                        last = pe.matmul(row4_ps[:, b:b + 1], alpha4_t[:, b, :], ones[:, 0:1], start=True, stop=True)
                    last.then_inc(S["row4_ps"], 1)
                if on[2]:
                    wait(pe, "h2t_hi", q, k, 2)
                    wait(pe, "h2t_lo", q, k, 2)
                    wait(pe, "y", q, k, 4, back=1)
                    weigh(res_ps, h2t_hi, h2t_lo, WSELF, True, False)
                    wait(pe, "agg2_lo", q, k, 2)
                    weigh(res_ps, agg_hi[:, 2], agg_lo[:, 2], WAGG, False).then_inc(S["res2_ps"], 1)
                if on[3]:
                    wait(pe, "agg3_lo", q, k, 3)
                    pe.matmul(gcn_ps, ones_r[0:2, :], bias_l2[:, :].unsqueeze(1).to_broadcast([2, G, feat]),
                              start=True, stop=False, skip_group_check=True)
                    weigh(gcn_ps, agg_hi[:, 3], agg_lo[:, 3], WGCN, False).then_inc(S["res3_ps"], 1)
                if on[1]:
                    if on[0]:
                        wait(pe, "z0", q, k, 0)
                    elif on[4]:
                        wait(pe, "th", q, k, 4)
                    wait(pe, "adj_mean", q, k, 1)
                    turn_pair(lambda b: adj_mean[:, b, :]).then_inc(S["adj_mean_t_ps"], 1)
                if on[4]:
                    wait(pe, "agg4_lo", q, k, 4)
                    if on[2]:
                        wait(pe, "x2", q, k, 2)
                    else:
                        wait(pe, "y", q, k, 4, back=1)
                    weigh(res_ps, agg_hi[:, 4], agg_lo[:, 4], WATT, True).then_inc(S["res4_ps"], 1)
                if on[1]:
                    if on[3]:
                        wait(pe, "x3", q, k, 3)
                    wait(pe, "adj_gcn", q, k, 1)
                    for b in range(G):
                        last = pe.transpose(gcn_t_ps[:, b, :], adj_gcn[:, b, :], ident[:, :])
                    last.then_inc(S["adj_gcn_t_ps"], 1)

            steps(pe, step)


def kernel(x, adj, L0_gnn_Wv, L0_gnn_bv, L0_gnn_aw, L0_gnn_ab, L0_gnn_Wk, L0_gnn_bk, L1_gnn_W, L2_gnn_kernel,
           L2_gnn_bias, L3_gnn_w, L3_gnn_a):
    import numpy as _np
    import concourse.bacc as _bacc
    from concourse import mybir as _mybir
    from concourse.bass_utils import run_bass_kernel_spmd as _run

    nc = _bacc.Bacc("TRN2", target_bir_lowering=False, num_devices=1)
    chunks = x.shape[2] // P
    aw_rows = _np.asarray(L0_gnn_aw).reshape(2, chunks, P).transpose(2, 1, 0)
    bv_rows = _np.asarray(L0_gnn_bv).reshape(chunks, P).T
    a_rows = _np.asarray(L3_gnn_a).reshape(chunks, P).T
    laid_out = {
        "x": x, "adj": adj, "wv_t": L0_gnn_Wv.T, "bv": bv_rows, "aw": aw_rows, "ab": L0_gnn_ab,
        "wk": L0_gnn_Wk, "bk": L0_gnn_bk, "w_cat_t": L1_gnn_W.T, "w_gcn": L2_gnn_kernel, "b_gcn": L2_gnn_bias,
        "w_att": L3_gnn_w, "w_att_t": L3_gnn_w.T, "a_att": a_rows,
    }
    arrays, args = {}, []
    for name, a in laid_out.items():
        a = _np.ascontiguousarray(a)
        arrays[f"in_{name}"] = a
        args.append(nc.dram_tensor(f"in_{name}", a.shape, _mybir.dt.from_np(a.dtype), kind="ExternalInput").ap())
    args.append(nc.dram_tensor("out", x.shape, _mybir.dt.float32, kind="ExternalOutput").ap())
    graph_layers(nc, *args)
    r = _run(nc, [arrays], core_ids=[0])
    return r.results[0]["out"]
```

```python
from contextlib import ExitStack

import concourse.bass as bass
from concourse import mybir

F32 = mybir.dt.float32
F32R = mybir.dt.float32r
ALU = mybir.AluOpType
ACT = mybir.ActivationFunctionType
AX = mybir.AxisListType

P = 128
G = 2
STAGES = 5
NORMS = 5
RING = 4
LN_EPS = 1e-5
SUM_EPS = 1e-12
DEG_EPS = 1e-6
SCALE = 8.0
W0, W1, W2, WSELF, WAGG, WGCN, WATT = range(7)
USE = [W2, W1, W0, WAGG, WSELF, WGCN, WATT]


def graph_layers(nc, x, adj, wv_t, bv, aw, ab, wk, bk, w_cat_t, w_gcn, b_gcn, w_att, w_att_t, a_att, out):
    n_graphs, nodes, feat = x.shape
    pairs = n_graphs // G
    chunks = feat // P
    width = G * feat
    n_bk = wk.shape[0]
    assert nodes == P and width == 512 and pairs % RING == 0

    x_d = x.rearrange("(q b) n d -> q n b d", b=G)
    adj_d = adj.rearrange("(q b) i j -> q i b j", b=G)
    out_d = out.rearrange("(q b) n d -> q n b d", b=G)

    with ExitStack() as ctx:
        def sb(name, shape, dt=F32):
            return ctx.enter_context(nc.sbuf_tensor(name, shape, dt))

        def sem(name):
            return ctx.enter_context(nc.semaphore(name))

        ones = sb("ones", [P, P])
        ident = sb("ident", [P, P])
        minus_half = sb("minus_half", [P, G])
        minus_one = sb("minus_one", [P, G])
        ln_eps = sb("ln_eps", [P, G])
        wts = sb("wts", [P, 7, chunks, feat])
        wts_hi = sb("wts_hi", [P, 7, chunks, feat], F32R)
        wts_lo = sb("wts_lo", [P, 7, chunks, feat], F32R)
        wv_t_sb = sb("wv_t_sb", [P, chunks, feat])
        w_att_t_sb = sb("w_att_t_sb", [P, chunks, feat])
        aw_sb = sb("aw_sb", [P, chunks, 2])
        bv_sb = sb("bv_sb", [P, chunks])
        ab_sb = sb("ab_sb", [1, 1])
        a_att_sb = sb("a_att_sb", [P, chunks])
        rows = sb("rows", [P, 4, feat])
        uj_row, ui_row, wa_row, gcn_bias_row = (rows[:, n, :] for n in range(4))
        score_const = sb("score_const", [P, G])
        b_gcn_sb = sb("b_gcn_sb", [1, feat])
        bias_f32 = sb("bias_f32", [n_bk, feat])
        bias_hi = sb("bias_hi", [n_bk, feat], F32R)
        bias_lo = sb("bias_lo", [n_bk, feat], F32R)
        bias_l0 = sb("bias_l0", [2 * n_bk, feat], F32R)
        ones_r = sb("ones_r", [2 * n_bk, P], F32R)

        x0 = sb("x0", [P, RING, G, feat])
        x1 = sb("x1", [P, 2, G, feat])
        x2 = sb("x2", [P, 2, G, feat])
        x3 = sb("x3", [P, 2, G, feat])
        y = sb("y", [P, 2, G, feat])
        adj_sb = sb("adj_sb", [P, RING, G, P])

        stats = sb("stats", [P, NORMS, G, 6])
        moments = sb("moments", [P, NORMS, G, 2])
        var_eps = sb("var_eps", [P, NORMS, G])
        rstd = sb("rstd", [P, NORMS, G])
        neg_mean = sb("neg_mean", [P, NORMS, G])
        shift = sb("shift", [P, NORMS, G])
        gcn_scale = sb("gcn_scale", [P, G])
        gcn_shift = sb("gcn_shift", [P, G])
        h = sb("h", [P, NORMS, G, feat])

        h0t_hi = sb("h0t_hi", [P, 2, chunks, G, P], F32R)
        h0t_lo = sb("h0t_lo", [P, 2, chunks, G, P], F32R)
        s0_bias = sb("s0_bias", [P, G])
        s0 = sb("s0", [P, G, 2])
        z0 = sb("z0", [P, G, P])
        lz0 = sb("lz0", [P, G, P])
        e0 = sb("e0", [P, G, P])
        alpha0 = sb("alpha0", [P, G, P])
        row0 = sb("row0", [P, G])
        rrow0 = sb("rrow0", [P, G])
        trans = sb("trans", [P, 2, G, P])
        deg = sb("deg", [P, RING, G])
        deg_max = sb("deg_max", [P, G])
        rdeg = sb("rdeg", [P, G])
        deg_1 = sb("deg_1", [P, G])
        dh = sb("dh", [P, RING, G])
        adj_mean = sb("adj_mean", [P, RING, G, P])
        self_mean = sb("self_mean", [P, G, P])
        gcn_rescale = sb("gcn_rescale", [P, RING, G])
        adj_mean_t = sb("adj_mean_t", [P, RING, G, P])
        adj_gcn_t = sb("adj_gcn_t", [P, 2, G, P])
        trans_t = sb("trans_t", [P, G, P])
        hw2 = sb("hw2", [P, G, feat])
        inner = sb("inner", [P, G, feat])
        h2t_hi = sb("h2t_hi", [P, chunks, G, P], F32R)
        h2t_lo = sb("h2t_lo", [P, chunks, G, P], F32R)
        hw_agg = sb("hw_agg", [P, G, feat])
        gcn_pre = sb("gcn_pre", [P, G, feat])
        agg_hi = sb("agg_hi", [P, 2, chunks, G, P], F32R)
        agg_lo = sb("agg_lo", [P, 2, chunks, G, P], F32R)
        unused0 = sb("unused0", [P, G, 2, feat])
        unused4 = sb("unused4", [P, G, feat])
        unused_row4 = sb("unused_row4", [P, G, P])
        s4 = sb("s4", [P, G])
        th = sb("th", [P, G, P])
        lth = sb("lth", [P, G, P])
        e4 = sb("e4", [P, G, P])
        alpha4_t = sb("alpha4_t", [P, G, P])
        row4 = sb("row4", [P, G])
        rrow4 = sb("rrow4", [P, G])
        scale4 = sb("scale4", [P, G])

        banks = ctx.enter_context(nc.psum_tensor("banks", [P, 8, width], F32))

        def cols(bank, inner_width):
            return banks[:, bank, 0:G * inner_width].rearrange("p (b d) -> p b d", b=G)

        def turned(bank):
            return banks[:, bank, :].rearrange("p (c b n) -> p c b n", c=chunks, b=G)

        hw2_ps = cols(0, feat)
        inner_ps = cols(1, feat)
        outer_ps = cols(2, feat)
        turn_ps = turned(3)
        hw_agg_ps = cols(4, feat)
        agg_ps, res2_ps = turned(5), cols(5, feat)
        pair_ps = cols(6, P)
        gcn_agg_ps, gcn_ps, res4_ps = turned(7), cols(7, feat), cols(7, feat)
        score_rows_ps = cols(7, feat)
        score_const_ps = banks[:, 5, 0:1]
        late_rows_ps = cols(4, feat)

        x_landed = [sem(f"x_landed{r}") for r in range(RING)]
        adj_landed = [sem(f"adj_landed{r}") for r in range(RING)]
        w_landed = [sem(f"w_landed{w}") for w in range(7)]
        y_stored = [sem(f"y_stored{r}") for r in range(2)]
        done = {name: sem(name) for name in (
            "score_in", "late_in", "bias_in", "bias_split", "bias_moved", "const_made", "ones_r", "rows_ps",
            "const_ps", "rows", "wts_hi", "wts_lo",
            *[f"{e}{s}" for s in (0, 2, 3, 4)
              for e in ("stats_", "moments_", "vareps_", "rstd_", "negm_", "shift_", "h_")],
            "gcnscale_", "gcnshift_",
            "h0t_ps", "h0t_hi", "h0t_lo", "s0", "s0_bias", "s0_row", "z0", "lz0", "e0", "alpha0", "rrow0",
            "trans",
            "deg", "degmax", "deg1", "rdeg", "dh", "gcn_rescale", "adj_mean", "self_mean",
            "adj_mean_t_ps", "adj_mean_t", "adj_gcn_t", "trans_t_ps", "trans_t",
            "hw2_ps", "hw2", "inner_ps", "inner", "outer_ps", "x1",
            "h2t_ps", "h2t_hi", "h2t_lo", "hw_agg_ps", "hw_agg", "res2_ps", "x2",
            "agg3_ps", "agg3_hi", "agg3_lo", "res3_ps", "gcn_pre", "x3",
            "s4", "s4_row", "th", "lth", "e4", "alpha4", "row4", "rrow4", "scale4",
            "agg4_ps", "agg4_hi", "agg4_lo", "res4_ps", "y")}

        def steps(engine, step, before=None):
            def written_out(first, end):
                for t in range(first, end):
                    if before and t in before:
                        before[t]()
                    step(t // RING, t % RING, {s: 0 <= t - s < pairs for s in range(-1, STAGES)})

            written_out(-1, 2 * RING)
            with engine.Fori(2, pairs // RING - 1) as q:
                for k in range(RING):
                    step(q, k, {s: True for s in range(-1, STAGES)})
            written_out(pairs - RING, pairs + STAGES - 1)

        def nth(q, k, stage, back=0):
            count = RING * q + (k - stage - back + 1)
            if isinstance(count, int):
                return min(count, pairs) if count > 0 else None
            return count

        def slot_nth(q, k, stage, ring, back=0):
            at = k - stage - back
            count = 16 * ((RING // ring) * q + (at // ring + 1))
            return at % ring, (None if isinstance(count, int) and count <= 0 else count)

        def slot(k, stage, ring):
            return (k - stage) % ring

        block = ctx.enter_context(nc.Block())

        @block.sync
        def _(sp):
            def load(q, k):
                r = slot(k, 0, RING)
                if (n := nth(q, k, 0, back=RING)) is not None:
                    sp.wait_ge(done["x1"], n)
                sp.dma_start(x0[:, r, :, :], x_d[RING * q + k]).then_inc(x_landed[r], 16)
                if (n := nth(q, k, 0, back=RING)) is not None:
                    sp.wait_ge(done["adj_mean"], n)
                sp.dma_start(adj_sb[:, r, :, :], adj_d[RING * q + k]).then_inc(adj_landed[r], 16)

            load(0, 0)
            for dst, src in ((aw_sb[:, :, :], aw), (bv_sb[:, :], bv), (ab_sb[:, :], ab.rearrange("(a b) -> a b", a=1)),
                             (wv_t_sb[:, :, :], wv_t.rearrange("(c p) d -> p c d", p=P))):
                sp.dma_start(dst, src).then_inc(done["score_in"], 16)
            for w, src in ((W2, wk[2]), (W1, wk[1])):
                sp.dma_start(wts[:, w, :, :], src.rearrange("(c p) o -> p c o", p=P)).then_inc(w_landed[w], 16)
            sp.dma_start(bias_f32[:, :], bk).then_inc(done["bias_in"], 16)
            load(0, 1)
            for w, src in ((W0, wk[0]), (WAGG, w_cat_t[feat:]), (WSELF, w_cat_t[:feat]), (WGCN, w_gcn), (WATT, w_att)):
                sp.dma_start(wts[:, w, :, :], src.rearrange("(c p) o -> p c o", p=P)).then_inc(w_landed[w], 16)
            for dst, src in ((b_gcn_sb[:, :], b_gcn.rearrange("(a b) -> a b", a=1)), (a_att_sb[:, :], a_att),
                             (w_att_t_sb[:, :, :], w_att_t.rearrange("(c p) d -> p c d", p=P))):
                sp.dma_start(dst, src).then_inc(done["late_in"], 16)
            sp.wait_ge(done["bias_split"], 2)
            sp.dma_start(bias_l0[0:n_bk, :].bitcast(F32), bias_hi[:, :].bitcast(F32)).then_inc(done["bias_moved"], 16)
            sp.dma_start(bias_l0[n_bk:2 * n_bk, :].bitcast(F32), bias_lo[:, :].bitcast(F32))\
                .then_inc(done["bias_moved"], 16)

            def step(q, k, on):
                if not isinstance(q, int) or 0 <= RING * q + k + 3 < pairs:
                    load(q, k + 3)
                if on[4]:
                    r = slot(k, 4, 2)
                    sp.wait_ge(done["y"], nth(q, k, 4))
                    sp.dma_start(out_d[RING * q + (k - 4)], y[:, r, :, :]).then_inc(y_stored[r], 16)

            steps(sp, step)
            for r in range(2):
                sp.wait_ge(y_stored[r], 16 * (pairs // 2))

        @block.gpsimd
        def _(pool):
            pool.memset(ones[:, :], 1.0).then_inc(done["const_made"], 1)
            pool.memset(minus_half[:, :], -0.5).then_inc(done["const_made"], 1)
            pool.memset(minus_one[:, :], -1.0).then_inc(done["const_made"], 1)
            pool.memset(ln_eps[:, :], LN_EPS).then_inc(done["const_made"], 1)
            pool.wait_ge(done["const_made"], 4)
            pool.affine_select(out=ident[:, :], in_=ones[:, :], compare_op=ALU.is_equal, fill=0.0, base=0,
                               pattern=[[-1, P]], channel_multiplier=1).then_inc(done["const_made"], 1)
            pool.wait_ge(done["const_made"], 5)

            def per_row(v):
                return v.unsqueeze(2).to_broadcast([P, G, P])

            def norm(q, k, s, at):
                pool.wait_ge(done[f"moments_{s}"], nth(q, k, at))
                if (n := nth(q, k, at, back=1)) is not None:
                    pool.wait_ge(done[f"h_{s}"], n)
                pool.tensor_tensor(var_eps[:, s, :], moments[:, s, :, 1], ln_eps[:, :], ALU.add)\
                    .then_inc(done[f"vareps_{s}"], 1)
                pool.tensor_tensor(neg_mean[:, s, :], moments[:, s, :, 0], minus_one[:, :], ALU.mult)\
                    .then_inc(done[f"negm_{s}"], 1)
                pool.wait_ge(done[f"vareps_{s}"], nth(q, k, at))
                pool.tensor_tensor(rstd[:, s, :], var_eps[:, s, :], minus_half[:, :], ALU.pow)\
                    .then_inc(done[f"rstd_{s}"], 1)
                pool.wait_ge(done[f"negm_{s}"], nth(q, k, at))
                pool.wait_ge(done[f"rstd_{s}"], nth(q, k, at))
                pool.tensor_tensor(shift[:, s, :], neg_mean[:, s, :], rstd[:, s, :], ALU.mult)\
                    .then_inc(done[f"shift_{s}"], 1)
                if s == 3:
                    r = slot(k, at, RING)
                    pool.wait_ge(done["shift_3"], nth(q, k, at))
                    pool.tensor_tensor(gcn_scale[:, :], rstd[:, 3, :], dh[:, r, :], ALU.mult)\
                        .then_inc(done["gcnscale_"], 1)
                    pool.tensor_tensor(gcn_shift[:, :], shift[:, 3, :], dh[:, r, :], ALU.mult)\
                        .then_inc(done["gcnshift_"], 1)

            def step(q, k, on):
                if on[1]:
                    pool.wait_ge(done["rrow0"], nth(q, k, 1))
                    if (n := nth(q, k, 1, back=2)) is not None:
                        pool.wait_ge(done["trans_t_ps"], n)
                    pool.tensor_tensor(trans[:, slot(k, 1, 2), :, :], alpha0[:, :, :], per_row(rrow0[:, :]),
                                       ALU.mult).then_inc(done["trans"], 1)
                if on[2]:
                    pool.wait_ge(done["self_mean"], nth(q, k, 2))
                    if (n := nth(q, k, 2, back=2)) is not None:
                        pool.wait_ge(done["agg3_ps"], n)
                    pool.wait_ge(done["adj_mean_t"], nth(q, k, 2))
                    pool.tensor_tensor(adj_gcn_t[:, slot(k, 2, 2), :, :], adj_mean_t[:, slot(k, 2, RING), :, :],
                                       self_mean[:, :, :], ALU.add).then_inc(done["adj_gcn_t"], 1)
                if on[-1]:
                    norm(q, k, 0, -1)
                if on[1]:
                    r = slot(k, 1, RING)
                    pool.wait_ge(done["deg"], nth(q, k, 1))
                    pool.tensor_tensor(deg_1[:, :], deg[:, r, :], ones[:, 0:G], ALU.add).then_inc(done["deg1"], 1)
                    pool.wait_ge(done["deg1"], nth(q, k, 1))
                    pool.tensor_tensor(dh[:, r, :], deg_1[:, :], minus_half[:, :], ALU.pow).then_inc(done["dh"], 1)
                    if (n := nth(q, k, 1, back=RING)) is not None:
                        pool.wait_ge(done["row4"], n)
                        pool.wait_ge(done["adj_mean_t_ps"], n)
                    pool.wait_ge(done["rdeg"], nth(q, k, 1))
                    pool.tensor_tensor(adj_mean[:, r, :, :], adj_sb[:, r, :, :], per_row(rdeg[:, :]), ALU.mult)\
                        .then_inc(done["adj_mean"], 1)
                    if (n := nth(q, k, 1, back=1)) is not None:
                        pool.wait_ge(done["adj_gcn_t"], n)
                    pool.tensor_tensor(self_mean[:, :, :], ident[:, :].unsqueeze(1).to_broadcast([P, G, P]),
                                       per_row(rdeg[:, :]), ALU.mult).then_inc(done["self_mean"], 1)
                    pool.wait_ge(done["dh"], nth(q, k, 1))
                    pool.tensor_tensor(gcn_rescale[:, r, :], dh[:, r, :], deg_max[:, :], ALU.mult)\
                        .then_inc(done["gcn_rescale"], 1)
                if on[3]:
                    norm(q, k, 4, 3)
                if on[2]:
                    norm(q, k, 3, 2)
                if on[1]:
                    norm(q, k, 2, 1)

            steps(pool, step)

        @block.scalar
        def _(act):
            def normalise(q, k, s, at):
                src, ring = {0: (x0, RING), 2: (x1, 2), 3: (x2, 2), 4: (x3, 2)}[s]
                scale, bias = (gcn_scale, gcn_shift) if s == 3 else (rstd[:, s, :], shift[:, s, :])
                act.wait_ge(done["gcnshift_" if s == 3 else f"shift_{s}"], nth(q, k, at))
                if s in (0, 2):
                    if (n := nth(q, k, at, back=1)) is not None:
                        act.wait_ge(done[f"h{s}t_ps"], n)
                if s > 2:
                    if (n := nth(q, k, at, back=1)) is not None:
                        act.wait_ge(done[f"agg{s}_ps"], n)
                if s in (0, 4):
                    if (n := nth(q, k, at, back=1)) is not None:
                        act.wait_ge(done[f"s{s}"], n)
                for b in range(G):
                    last = act.activation(h[:, s, b, :], src[:, slot(k, at, ring), b, :], ACT.Relu,
                                          bias=bias[:, b:b + 1], scale=scale[:, b:b + 1])
                last.then_inc(done[f"h_{s}"], 1)

            def agg_hi_copy(q, k, s, ps):
                act.wait_ge(done[f"agg{s}_ps"], nth(q, k, s))
                if (n := nth(q, k, s, back=1)) is not None:
                    act.wait_ge(done[f"res{s}_ps"], n)
                act.copy(agg_hi[:, s - 3, :, :, :], ps).then_inc(done[f"agg{s}_hi"], 1)

            def step(q, k, on):
                if on[4]:
                    act.wait_ge(done["s4_row"], nth(q, k, 4))
                    if (n := nth(q, k, 4, back=1)) is not None:
                        act.wait_ge(done["lth"], n)
                    for b in range(G):
                        last = act.activation(th[:, b, :], pair_ps[:, b, :], ACT.Tanh, bias=s4[:, b:b + 1])
                    last.then_inc(done["th"], 1)
                if on[3]:
                    normalise(q, k, 3, 3)
                if on[1]:
                    act.wait_ge(done["hw2_ps"], nth(q, k, 1))
                    if (n := nth(q, k, 1, back=1)) is not None:
                        act.wait_ge(done["inner_ps"], n)
                    act.copy(hw2[:, :, :], hw2_ps).then_inc(done["hw2"], 1)
                if on[4]:
                    act.wait_ge(done["lth"], nth(q, k, 4))
                    if (n := nth(q, k, 4, back=1)) is not None:
                        act.wait_ge(done["alpha4"], n)
                        act.wait_ge(done["row4"], n)
                    act.activation(e4[:, :, :], lth[:, :, :], ACT.Exp, scale=SCALE).then_inc(done["e4"], 1)
                if on[2]:
                    normalise(q, k, 2, 2)
                if on[3]:
                    agg_hi_copy(q, k, 3, gcn_agg_ps)
                if on[1]:
                    act.wait_ge(done["trans_t_ps"], nth(q, k, 1))
                    if (n := nth(q, k, 1, back=1)) is not None:
                        act.wait_ge(done["outer_ps"], n)
                    act.copy(trans_t[:, :, :], pair_ps).then_inc(done["trans_t"], 1)
                if on[4]:
                    agg_hi_copy(q, k, 4, agg_ps)
                if on[2]:
                    act.wait_ge(done["h2t_ps"], nth(q, k, 2))
                    if (n := nth(q, k, 2, back=1)) is not None:
                        act.wait_ge(done["res2_ps"], n)
                    act.copy(h2t_hi[:, :, :, :], turn_ps).then_inc(done["h2t_hi"], 1)
                if on[0]:
                    normalise(q, k, 0, 0)
                if on[2]:
                    act.wait_ge(done["hw_agg_ps"], nth(q, k, 2))
                    if (n := nth(q, k, 2, back=1)) is not None:
                        act.wait_ge(done["res2_ps"], n)
                    act.copy(hw_agg[:, :, :], hw_agg_ps).then_inc(done["hw_agg"], 1)
                if on[1]:
                    act.wait_ge(done["inner_ps"], nth(q, k, 1))
                    if (n := nth(q, k, 1, back=1)) is not None:
                        act.wait_ge(done["outer_ps"], n)
                    act.copy(inner[:, :, :], inner_ps).then_inc(done["inner"], 1)
                if on[0]:
                    act.wait_ge(done["h0t_ps"], nth(q, k, 0))
                    if (n := nth(q, k, 0, back=2)) is not None:
                        act.wait_ge(done["outer_ps"], n)
                    act.copy(h0t_hi[:, slot(k, 0, 2), :, :, :], turn_ps).then_inc(done["h0t_hi"], 1)
                if on[1]:
                    if (n := nth(q, k, 1, back=RING)) is not None:
                        act.wait_ge(done["res2_ps"], n)
                        act.wait_ge(done["adj_gcn_t"], n)
                        act.wait_ge(done["alpha4"], n)
                    act.wait_ge(done["adj_mean_t_ps"], nth(q, k, 1))
                    act.copy(adj_mean_t[:, slot(k, 1, RING), :, :], pair_ps).then_inc(done["adj_mean_t"], 1)
                if on[3]:
                    normalise(q, k, 4, 3)
                if on[0]:
                    act.wait_ge(done["s0_bias"], nth(q, k, 0))
                    if (n := nth(q, k, 0, back=1)) is not None:
                        act.wait_ge(done["lz0"], n)
                    act.wait_ge(done["s0_row"], nth(q, k, 0))
                    for b in range(G):
                        last = act.activation(z0[:, b, :], pair_ps[:, b, :], ACT.Identity, bias=s0_bias[:, b:b + 1])
                    last.then_inc(done["z0"], 1)
                if on[0]:
                    act.wait_ge(done["lz0"], nth(q, k, 0))
                    if (n := nth(q, k, 0, back=1)) is not None:
                        act.wait_ge(done["alpha0"], n)
                    act.activation(e0[:, :, :], lz0[:, :, :], ACT.Exp).then_inc(done["e0"], 1)

            steps(act, step)

        @block.vector
        def _(dve):
            def split(*weights):
                for w in weights:
                    n = USE.index(w) + 1
                    dve.wait_ge(w_landed[w], 16)
                    dve.tensor_copy(wts_hi[:, w, :, :], wts[:, w, :, :]).then_inc(done["wts_hi"], 1)
                    dve.wait_ge(done["wts_hi"], n)
                    dve.tensor_tensor(wts_lo[:, w, :, :], wts[:, w, :, :], wts_hi[:, w, :, :].bitcast(F32),
                                      ALU.subtract).then_inc(done["wts_lo"], 1)

            def before_step_0():
                dve.wait_ge(done["const_made"], 5)
                dve.tensor_copy(ones_r[:, :], ones[0:2 * n_bk, :]).then_inc(done["ones_r"], 1)
                split(W2)
                dve.wait_ge(done["bias_in"], 16)
                dve.tensor_copy(bias_hi[:, :], bias_f32[:, :]).then_inc(done["bias_split"], 1)
                dve.wait_ge(done["bias_split"], 1)
                dve.tensor_tensor(bias_lo[:, :], bias_f32[:, :], bias_hi[:, :].bitcast(F32), ALU.subtract)\
                    .then_inc(done["bias_split"], 1)
                split(W1, W0)
                dve.wait_ge(done["rows_ps"], 1)
                dve.tensor_copy(rows[:, 0:2, :], score_rows_ps).then_inc(done["rows"], 1)
                dve.wait_ge(done["const_ps"], 1)
                for b in range(G):
                    dve.tensor_copy(score_const[:, b:b + 1], score_const_ps)
                dve.wait_ge(done["rows"], 1)

            def before_step_2():
                dve.wait_ge(done["rows_ps"], 2)
                dve.tensor_copy(rows[:, 2:4, :], late_rows_ps).then_inc(done["rows"], 1)
                split(WGCN, WATT)
                dve.wait_ge(done["rows"], 2)

            def stats_of(q, k, s, at):
                src, ring = {0: (x0, RING), 2: (x1, 2), 3: (x2, 2), 4: (x3, 2)}[s]
                if (n := nth(q, k, at, back=1)) is not None:
                    dve.wait_ge(done[f"moments_{s}"], n)
                if s == 0:
                    r, n = slot_nth(q, k, at, RING)
                    dve.wait_ge(x_landed[r], n)
                else:
                    dve.wait_ge(done[f"x{s - 1}"], nth(q, k, at))
                for b in range(G):
                    last = dve.bn_stats(stats[:, s, b, :], src[:, slot(k, at, ring), b, :])
                last.then_inc(done[f"stats_{s}"], 1)

            def wait_moments(q, k, s, at):
                if (n := nth(q, k, at, back=1)) is not None:
                    dve.wait_ge(done[f"negm_{s}"], n)
                    dve.wait_ge(done[f"vareps_{s}"], n)
                dve.wait_ge(done[f"stats_{s}"], nth(q, k, at))

            def moments_of(s):
                for b in range(G):
                    last = dve.bn_aggr(moments[:, s, b, :], stats[:, s, b, :])
                last.then_inc(done[f"moments_{s}"], 1)

            def agg_lo_sub(q, k, s, ps):
                dve.wait_ge(done[f"agg{s}_hi"], nth(q, k, s))
                if (n := nth(q, k, s, back=1)) is not None:
                    dve.wait_ge(done[f"res{s}_ps"], n)
                dve.tensor_tensor(agg_lo[:, s - 3, :, :, :], ps, agg_hi[:, s - 3, :, :, :].bitcast(F32), ALU.subtract)\
                    .then_inc(done[f"agg{s}_lo"], 1)

            def residual(q, k, s, ps, src, src_ring, dst, name):
                if (n := nth(q, k, s, back=2)) is not None:
                    dve.wait_ge(done[f"h_{s + 1}"], n)
                dve.wait_ge(done[{1: "outer_ps", 2: "res2_ps", 3: "gcn_pre"}[s]], nth(q, k, s))
                dve.scalar_tensor_tensor(out=dst[:, slot(k, s, 2), :, :], in0=ps, scalar=0.0,
                                         in1=src[:, slot(k, s, src_ring), :, :], op0=ALU.max, op1=ALU.add)\
                    .then_inc(done[name], 1)

            def score4(b):
                return dve.tensor_tensor_reduce(unused4[:, b, :], h[:, 4, b, :], wa_row, 1 / SCALE, 0.0,
                                                ALU.mult, ALU.add, s4[:, b:b + 1])

            def attend0(k, b):
                return dve.tensor_tensor_reduce(alpha0[:, b, :], e0[:, b, :], adj_sb[:, slot(k, 0, RING), b, :], 1.0,
                                                SUM_EPS, ALU.mult, ALU.add, row0[:, b:b + 1])

            def score0(b, j):
                return dve.tensor_tensor_reduce(unused0[:, b, j, :], h[:, 0, b, :], (uj_row, ui_row)[j], 1.0, 0.0,
                                                ALU.mult, ALU.add, s0[:, b, j:j + 1])

            def step(q, k, on):
                if on[4]:
                    if (n := nth(q, k, 4, back=1)) is not None:
                        dve.wait_ge(done["e4"], n)
                    dve.wait_ge(done["th"], nth(q, k, 4))
                    dve.scalar_tensor_tensor(out=lth[:, :, :], in0=th[:, :, :], scalar=0.1, in1=th[:, :, :],
                                             op0=ALU.mult, op1=ALU.max).then_inc(done["lth"], 1)
                if on[-1]:
                    stats_of(q, k, 0, -1)
                if on[4]:
                    if (n := nth(q, k, 4, back=1)) is not None:
                        dve.wait_ge(done["agg4_ps"], n)
                    dve.wait_ge(done["adj_mean_t"], nth(q, k, 4))
                    dve.wait_ge(done["e4"], nth(q, k, 4))
                    dve.tensor_tensor(alpha4_t[:, :, :], e4[:, :, :], adj_mean_t[:, slot(k, 4, RING), :, :],
                                      ALU.mult).then_inc(done["alpha4"], 1)
                if on[-1]:
                    wait_moments(q, k, 0, -1)
                if on[3]:
                    agg_lo_sub(q, k, 3, gcn_agg_ps)
                if on[-1]:
                    moments_of(0)
                if on[4]:
                    if (n := nth(q, k, 4, back=1)) is not None:
                        dve.wait_ge(done["rrow4"], n)
                    dve.wait_ge(done["adj_mean"], nth(q, k, 4))
                    for b in range(G):
                        last = dve.tensor_tensor_reduce(unused_row4[:, b, :], e4[:, b, :],
                                                        adj_mean[:, slot(k, 4, RING), b, :], 1.0, 0.0,
                                                        ALU.mult, ALU.add, row4[:, b:b + 1])
                    last.then_inc(done["row4"], 1)
                if on[1]:
                    r, n = slot_nth(q, k, 1, RING)
                    dve.wait_ge(adj_landed[r], n)
                    dve.tensor_reduce(deg[:, slot(k, 1, RING), :], adj_sb[:, slot(k, 1, RING), :, :], AX.X, ALU.add)\
                        .then_inc(done["deg"], 1)
                if on[2]:
                    if (n := nth(q, k, 2, back=1)) is not None:
                        dve.wait_ge(done["res2_ps"], n)
                    dve.wait_ge(done["h2t_hi"], nth(q, k, 2))
                    dve.tensor_tensor(h2t_lo[:, :, :, :], turn_ps, h2t_hi[:, :, :, :].bitcast(F32), ALU.subtract)\
                        .then_inc(done["h2t_lo"], 1)
                if on[1]:
                    if (n := nth(q, k, 1, back=1)) is not None:
                        dve.wait_ge(done["gcn_rescale"], n)
                    dve.wait_ge(done["deg"], nth(q, k, 1))
                    dve.tensor_scalar(deg_max[:, :], deg[:, slot(k, 1, RING), :], DEG_EPS, None, ALU.max)\
                        .then_inc(done["degmax"], 1)
                if on[4]:
                    dve.wait_ge(done["row4"], nth(q, k, 4))
                    dve.reciprocal(rrow4[:, :], row4[:, :]).then_inc(done["rrow4"], 1)
                if on[4]:
                    agg_lo_sub(q, k, 4, agg_ps)
                if on[1]:
                    if (n := nth(q, k, 1, back=1)) is not None:
                        dve.wait_ge(done["adj_mean"], n)
                        dve.wait_ge(done["self_mean"], n)
                    dve.wait_ge(done["degmax"], nth(q, k, 1))
                    dve.reciprocal(rdeg[:, :], deg_max[:, :]).then_inc(done["rdeg"], 1)
                if on[3]:
                    dve.wait_ge(done["gcn_rescale"], nth(q, k, 3))
                    if (n := nth(q, k, 3, back=1)) is not None:
                        dve.wait_ge(done["x3"], n)
                    dve.wait_ge(done["res3_ps"], nth(q, k, 3))
                    for b in range(G):
                        last = dve.scalar_tensor_tensor(out=gcn_pre[:, b, :], in0=gcn_ps[:, b, :],
                                                        scalar=gcn_rescale[:, slot(k, 3, RING), b:b + 1],
                                                        in1=gcn_bias_row, op0=ALU.mult, op1=ALU.add)
                    last.then_inc(done["gcn_pre"], 1)
                if on[0]:
                    if (n := nth(q, k, 0, back=1)) is not None:
                        dve.wait_ge(done["s0_row"], n)
                        dve.wait_ge(done["s0_bias"], n)
                    dve.wait_ge(done["h_0"], nth(q, k, 0))
                    score0(0, 0)
                if on[3]:
                    residual(q, k, 3, gcn_pre[:, :, :], x2, 2, x3, "x3")
                if on[0]:
                    score0(0, 1)
                if on[3]:
                    stats_of(q, k, 4, 3)
                if on[0]:
                    score0(1, 0)
                if on[3]:
                    wait_moments(q, k, 4, 3)
                if on[4]:
                    dve.wait_ge(done["rrow4"], nth(q, k, 4))
                    dve.tensor_tensor(scale4[:, :], rrow4[:, :], deg[:, slot(k, 4, RING), :], ALU.mult)\
                        .then_inc(done["scale4"], 1)
                if on[3]:
                    moments_of(4)
                if on[0]:
                    score0(1, 1).then_inc(done["s0"], 1)
                if on[2]:
                    residual(q, k, 2, res2_ps, x1, 2, x2, "x2")
                if on[0]:
                    if (n := nth(q, k, 0, back=1)) is not None:
                        dve.wait_ge(done["z0"], n)
                    dve.wait_ge(done["s0"], nth(q, k, 0))
                    dve.tensor_tensor(s0_bias[:, :], s0[:, :, 1], score_const[:, :], ALU.add)\
                        .then_inc(done["s0_bias"], 1)
                if on[0]:
                    if (n := nth(q, k, 0, back=2)) is not None:
                        dve.wait_ge(done["outer_ps"], n)
                    dve.wait_ge(done["h0t_hi"], nth(q, k, 0))
                    dve.tensor_tensor(h0t_lo[:, slot(k, 0, 2), :, :, :], turn_ps,
                                      h0t_hi[:, slot(k, 0, 2), :, :, :].bitcast(F32), ALU.subtract)\
                        .then_inc(done["h0t_lo"], 1)
                if on[2]:
                    stats_of(q, k, 3, 2)
                if on[3]:
                    if (n := nth(q, k, 3, back=1)) is not None:
                        dve.wait_ge(done["s4_row"], n)
                    dve.wait_ge(done["h_4"], nth(q, k, 3))
                    score4(0)
                if on[2]:
                    wait_moments(q, k, 3, 2)
                if on[3]:
                    score4(1).then_inc(done["s4"], 1)
                if on[2]:
                    moments_of(3)
                if on[1]:
                    residual(q, k, 1, outer_ps, x0, RING, x1, "x1")
                if on[0]:
                    if (n := nth(q, k, 0, back=1)) is not None:
                        dve.wait_ge(done["e0"], n)
                    dve.wait_ge(done["z0"], nth(q, k, 0))
                    dve.scalar_tensor_tensor(out=lz0[:, :, :], in0=z0[:, :, :], scalar=0.2, in1=z0[:, :, :],
                                             op0=ALU.mult, op1=ALU.max).then_inc(done["lz0"], 1)
                if on[1]:
                    stats_of(q, k, 2, 1)
                if on[0]:
                    if (n := nth(q, k, 0, back=1)) is not None:
                        dve.wait_ge(done["trans"], n)
                    r, n = slot_nth(q, k, 0, RING)
                    dve.wait_ge(adj_landed[r], n)
                    dve.wait_ge(done["e0"], nth(q, k, 0))
                    attend0(k, 0)
                if on[1]:
                    wait_moments(q, k, 2, 1)
                if on[0]:
                    attend0(k, 1).then_inc(done["alpha0"], 1)
                if on[1]:
                    moments_of(2)
                if on[0]:
                    if (n := nth(q, k, 0, back=1)) is not None:
                        dve.wait_ge(done["trans"], n)
                    dve.wait_ge(done["alpha0"], nth(q, k, 0))
                    dve.reciprocal(rrow0[:, :], row0[:, :]).then_inc(done["rrow0"], 1)
                if on[4]:
                    dve.wait_ge(done["scale4"], nth(q, k, 4))
                    r, n = slot_nth(q, k, 4, 2, back=2)
                    if n is not None:
                        dve.wait_ge(y_stored[r], n)
                    dve.wait_ge(done["res4_ps"], nth(q, k, 4))
                    for b in range(G):
                        last = dve.scalar_tensor_tensor(out=y[:, slot(k, 4, 2), b, :], in0=res4_ps[:, b, :],
                                                        scalar=scale4[:, b:b + 1],
                                                        in1=x3[:, slot(k, 4, 2), b, :], op0=ALU.mult,
                                                        op1=ALU.add)
                    last.then_inc(done["y"], 1)

            steps(dve, step, {0: before_step_0, 1: lambda: split(WAGG, WSELF), 2: before_step_2})

        @block.tensor
        def _(pe):
            def row_sum(dst, column, matrix):
                for o in range(chunks):
                    last = pe.matmul(dst, column(o).to_broadcast([P, P]), matrix[:, o, :], start=(o == 0),
                                     stop=(o == chunks - 1), skip_group_check=True)
                return last

            pe.wait_ge(done["const_made"], 5)
            pe.wait_ge(done["score_in"], 16 * 4)
            for j in range(2):
                last = row_sum(score_rows_ps[:, j, :], lambda o: aw_sb[:, o, j:j + 1], wv_t_sb)
            last.then_inc(done["rows_ps"], 1)
            for o in range(chunks):
                for j in range(2):
                    pe.matmul(score_const_ps, bv_sb[:, o:o + 1].to_broadcast([P, P]), aw_sb[:, o, j:j + 1],
                              start=(o == 0 and j == 0), stop=False)
            pe.matmul(score_const_ps, ones[0:1, :], ab_sb[:, :], start=False, stop=True)\
                .then_inc(done["const_ps"], 1)

            def before_step_1():
                pe.wait_ge(done["late_in"], 16 * 3)
                row_sum(late_rows_ps[:, 0, :], lambda o: a_att_sb[:, o:o + 1], w_att_t_sb)
                pe.matmul(late_rows_ps[:, 1, :], ones[0:1, :], b_gcn_sb[:, :], start=True, stop=True)\
                    .then_inc(done["rows_ps"], 1)
                pe.wait_ge(done["ones_r"], 1)
                pe.wait_ge(done["bias_moved"], 16 * 2)

            split_waited = []

            def weigh(dst, hi, lo, w, first, closes=True):
                if w not in split_waited:
                    split_waited.append(w)
                    pe.wait_ge(done["wts_lo"], USE.index(w) + 1)
                for b in range(G):
                    for c in range(chunks):
                        for i, (left, right) in enumerate(((hi, wts_hi), (hi, wts_lo), (lo, wts_hi))):
                            last = pe.matmul(dst[:, b, :], left[:, c, b, :], right[:, w, c, :],
                                             start=(first and b == 0 and c == 0 and i == 0),
                                             stop=(closes and c == chunks - 1 and i == 2), skip_group_check=True)
                return last

            def turn_h(s):
                for c in range(chunks):
                    for b in range(G):
                        last = pe.transpose(turn_ps[:, c, b, :], h[:, s, b, c * P:(c + 1) * P], ident[:, :])
                return last

            def aggregate(dst, s, mat):
                for c in range(chunks):
                    for b in range(G):
                        last = pe.matmul(dst[:, c, b, :], h[:, s, b, c * P:(c + 1) * P], mat[:, b, :],
                                         start=True, stop=True)
                return last

            def turn_pair(src):
                for b in range(G):
                    last = pe.transpose(pair_ps[:, b, :], src(b), ident[:, :])
                return last

            def step(q, k, on):
                r0, r1 = slot(k, 0, 2), slot(k, 1, 2)
                if on[4]:
                    if on[1]:
                        pe.wait_ge(done["z0"], nth(q, k, 0, back=1))
                    else:
                        if (n := nth(q, k, 1, back=1)) is not None:
                            pe.wait_ge(done["adj_mean_t"], n)
                        if (n := nth(q, k, 4, back=1)) is not None:
                            pe.wait_ge(done["th"], n)
                    pe.wait_ge(done["s4"], nth(q, k, 4))
                    turn_pair(lambda b: s4[:, b:b + 1].to_broadcast([P, P])).then_inc(done["s4_row"], 1)
                if on[1]:
                    if (n := nth(q, k, 1, back=1)) is not None:
                        pe.wait_ge(done["inner"], n)
                    weigh(inner_ps, h0t_hi[:, r1], h0t_lo[:, r1], W1, True, False)
                if on[1]:
                    if (n := nth(q, k, 1, back=1)) is not None:
                        pe.wait_ge(done["x1"], n)
                    pe.matmul(outer_ps, ones_r[:, :],
                              bias_l0[:, :].unsqueeze(1).to_broadcast([2 * n_bk, G, feat]), start=True, stop=False,
                              skip_group_check=True)
                    weigh(outer_ps, h0t_hi[:, r1], h0t_lo[:, r1], W0, False, False)
                if on[3]:
                    if (n := nth(q, k, 4, back=1)) is not None:
                        pe.wait_ge(done["y"], n)
                    pe.wait_ge(done["adj_gcn_t"], nth(q, k, 3))
                    pe.wait_ge(done["h_3"], nth(q, k, 3))
                    aggregate(gcn_agg_ps, 3, adj_gcn_t[:, slot(k, 3, 2)]).then_inc(done["agg3_ps"], 1)
                if on[1]:
                    if on[4]:
                        pe.wait_ge(done["th"], nth(q, k, 4))
                    elif (n := nth(q, k, 0, back=1)) is not None:
                        pe.wait_ge(done["z0"], n)
                    pe.wait_ge(done["trans"], nth(q, k, 1))
                    turn_pair(lambda b: trans[:, r1, b, :]).then_inc(done["trans_t_ps"], 1)
                if on[4]:
                    if (n := nth(q, k, 2, back=1)) is not None:
                        pe.wait_ge(done["x2"], n)
                    pe.wait_ge(done["alpha4"], nth(q, k, 4))
                    aggregate(agg_ps, 4, alpha4_t).then_inc(done["agg4_ps"], 1)
                if on[2]:
                    if (n := nth(q, k, 0, back=1)) is not None:
                        pe.wait_ge(done["h0t_lo"], n)
                    pe.wait_ge(done["h_2"], nth(q, k, 2))
                    turn_h(2).then_inc(done["h2t_ps"], 1)
                if on[1]:
                    pe.wait_ge(done["trans_t"], nth(q, k, 1))
                    pe.wait_ge(done["hw2"], nth(q, k, 1))
                    for b in range(G):
                        last = pe.matmul(inner_ps[:, b, :], trans_t[:, b, :], hw2[:, b, :], start=False, stop=True,
                                         skip_group_check=True)
                    last.then_inc(done["inner_ps"], 1)
                if on[3]:
                    pe.wait_ge(done["agg3_lo"], nth(q, k, 3))
                    weigh(gcn_ps, agg_hi[:, 0], agg_lo[:, 0], WGCN, True).then_inc(done["res3_ps"], 1)
                if on[2]:
                    if (n := nth(q, k, 2, back=1)) is not None:
                        pe.wait_ge(done["hw_agg"], n)
                    pe.wait_ge(done["h2t_hi"], nth(q, k, 2))
                    pe.wait_ge(done["h2t_lo"], nth(q, k, 2))
                    weigh(hw_agg_ps, h2t_hi, h2t_lo, WAGG, True).then_inc(done["hw_agg_ps"], 1)
                if on[2]:
                    if on[4]:
                        pe.wait_ge(done["agg4_lo"], nth(q, k, 4))
                    elif (n := nth(q, k, 2, back=1)) is not None:
                        pe.wait_ge(done["x2"], n)
                    weigh(res2_ps, h2t_hi, h2t_lo, WSELF, True, False)
                if on[2]:
                    pe.wait_ge(done["adj_mean_t"], nth(q, k, 2))
                    pe.wait_ge(done["hw_agg"], nth(q, k, 2))
                    for b in range(G):
                        last = pe.matmul(res2_ps[:, b, :], adj_mean_t[:, slot(k, 2, RING), b, :], hw_agg[:, b, :],
                                         start=False, stop=True, skip_group_check=True)
                    last.then_inc(done["res2_ps"], 1)
                if on[0]:
                    if (n := nth(q, k, 2)) is not None:
                        pe.wait_ge(done["h2t_lo"], n)
                    pe.wait_ge(done["h_0"], nth(q, k, 0))
                    turn_h(0).then_inc(done["h0t_ps"], 1)
                if on[1]:
                    pe.wait_ge(done["trans_t"], nth(q, k, 1))
                    pe.wait_ge(done["adj_mean"], nth(q, k, 1))
                    turn_pair(lambda b: adj_mean[:, slot(k, 1, RING), b, :]).then_inc(done["adj_mean_t_ps"], 1)
                if on[4]:
                    if (n := nth(q, k, 3)) is not None:
                        pe.wait_ge(done["gcn_pre"], n)
                    pe.wait_ge(done["agg4_lo"], nth(q, k, 4))
                    weigh(res4_ps, agg_hi[:, 1], agg_lo[:, 1], WATT, True).then_inc(done["res4_ps"], 1)
                if on[1]:
                    pe.wait_ge(done["inner"], nth(q, k, 1))
                    for b in range(G):
                        last = pe.matmul(outer_ps[:, b, :], trans_t[:, b, :], inner[:, b, :], start=False, stop=True,
                                         skip_group_check=True)
                    last.then_inc(done["outer_ps"], 1)
                if on[0]:
                    if (n := nth(q, k, 1)) is not None:
                        pe.wait_ge(done["adj_mean_t"], n)
                    pe.wait_ge(done["s0"], nth(q, k, 0))
                    turn_pair(lambda b: s0[:, b, 0:1].to_broadcast([P, P])).then_inc(done["s0_row"], 1)
                if on[0]:
                    if (n := nth(q, k, 0, back=1)) is not None:
                        pe.wait_ge(done["hw2"], n)
                    pe.wait_ge(done["h0t_hi"], nth(q, k, 0))
                    pe.wait_ge(done["h0t_lo"], nth(q, k, 0))
                    weigh(hw2_ps, h0t_hi[:, r0], h0t_lo[:, r0], W2, True).then_inc(done["hw2_ps"], 1)

            steps(pe, step, {1: before_step_1, 2: lambda: pe.wait_ge(done["rows"], 2)})


def kernel(x, adj, L0_gnn_Wv, L0_gnn_bv, L0_gnn_aw, L0_gnn_ab, L0_gnn_Wk, L0_gnn_bk, L1_gnn_W, L2_gnn_kernel,
           L2_gnn_bias, L3_gnn_w, L3_gnn_a):
    import numpy as _np
    import concourse.bacc as _bacc
    from concourse import mybir as _mybir
    from concourse.bass_utils import run_bass_kernel_spmd as _run

    nc = _bacc.Bacc("TRN2", target_bir_lowering=False, num_devices=1)
    chunks = x.shape[2] // P
    aw_rows = _np.asarray(L0_gnn_aw).reshape(2, chunks, P).transpose(2, 1, 0)
    bv_rows = _np.asarray(L0_gnn_bv).reshape(chunks, P).T
    a_rows = _np.asarray(L3_gnn_a).reshape(chunks, P).T
    laid_out = {
        "x": x, "adj": adj, "wv_t": L0_gnn_Wv.T, "bv": bv_rows, "aw": aw_rows, "ab": L0_gnn_ab,
        "wk": L0_gnn_Wk, "bk": L0_gnn_bk, "w_cat_t": L1_gnn_W.T, "w_gcn": L2_gnn_kernel, "b_gcn": L2_gnn_bias,
        "w_att": L3_gnn_w, "w_att_t": L3_gnn_w.T, "a_att": a_rows,
    }
    arrays, args = {}, []
    for name, a in laid_out.items():
        a = _np.ascontiguousarray(a)
        arrays[f"in_{name}"] = a
        args.append(nc.dram_tensor(f"in_{name}", a.shape, _mybir.dt.from_np(a.dtype), kind="ExternalInput").ap())
    args.append(nc.dram_tensor("out", x.shape, _mybir.dt.float32, kind="ExternalOutput").ap())
    graph_layers(nc, *args)
    r = _run(nc, [arrays], core_ids=[0])
    return r.results[0]["out"]
```
